# Optimizing a Trainium2 kernel written in Bass

```python
import numpy as np
import jax
import jax.numpy as jnp

def _softmax(x, axis=-1):
    return jax.nn.softmax(x, axis=axis)

def _gelu(x):
    return jax.nn.gelu(x, approximate=True)

def _silu(x):
    return jax.nn.silu(x)

def _sigmoid(x):
    return jax.nn.sigmoid(x)

def _layernorm(x, axis=-1, eps=1e-05):
    m = jnp.mean(x, axis=axis, keepdims=True)
    v = jnp.var(x, axis=axis, keepdims=True)
    return (x - m) / jnp.sqrt(v + eps)

def _scatter_add(tgt, idx, src, axis=0):
    return tgt.at[idx].add(src)

def _segment_sum(src, seg, n):
    return jax.ops.segment_sum(src, seg, n)
kernel_name = 'mk_dlrm_tower_d1_rec_r8_7e53a9'

def setup_inputs(seed: int=0):
    np.random.seed(seed)
    _w = jnp.asarray

    def _rec_inputs():
        import jax
        import jax.numpy as jnp
        _tk = jax.random.key(seed)
        dense_ctx = jax.random.normal(jax.random.fold_in(_tk, 190), (1024, 16), jnp.float32)
        ids = jnp.stack([jax.random.randint(jax.random.fold_in(_tk, 200 + f), (1024,), 0, v, jnp.int32) for f, v in enumerate([1250, 1000, 1000, 12500, 12500, 1250, 1000, 12500, 12500, 1250, 125000, 1000, 1250, 125000, 1250, 125000, 1250, 125000, 125000, 125000, 1000, 1000, 12500, 1000, 1250, 1250, 1000, 12500, 1000, 1000, 125000, 1250])], axis=1)
        tbl_0 = 0.05 * jax.random.normal(jax.random.fold_in(_tk, 500 + 0), (1250, 16), jnp.float32)
        tbl_1 = 0.05 * jax.random.normal(jax.random.fold_in(_tk, 500 + 1), (1000, 16), jnp.float32)
        tbl_2 = 0.05 * jax.random.normal(jax.random.fold_in(_tk, 500 + 2), (1000, 16), jnp.float32)
        tbl_3 = 0.05 * jax.random.normal(jax.random.fold_in(_tk, 500 + 3), (12500, 16), jnp.float32)
        tbl_4 = 0.05 * jax.random.normal(jax.random.fold_in(_tk, 500 + 4), (12500, 16), jnp.float32)
        tbl_5 = 0.05 * jax.random.normal(jax.random.fold_in(_tk, 500 + 5), (1250, 16), jnp.float32)
        tbl_6 = 0.05 * jax.random.normal(jax.random.fold_in(_tk, 500 + 6), (1000, 16), jnp.float32)
        tbl_7 = 0.05 * jax.random.normal(jax.random.fold_in(_tk, 500 + 7), (12500, 16), jnp.float32)
        tbl_8 = 0.05 * jax.random.normal(jax.random.fold_in(_tk, 500 + 8), (12500, 16), jnp.float32)
        tbl_9 = 0.05 * jax.random.normal(jax.random.fold_in(_tk, 500 + 9), (1250, 16), jnp.float32)
        tbl_10 = 0.05 * jax.random.normal(jax.random.fold_in(_tk, 500 + 10), (125000, 16), jnp.float32)
        tbl_11 = 0.05 * jax.random.normal(jax.random.fold_in(_tk, 500 + 11), (1000, 16), jnp.float32)
        tbl_12 = 0.05 * jax.random.normal(jax.random.fold_in(_tk, 500 + 12), (1250, 16), jnp.float32)
        tbl_13 = 0.05 * jax.random.normal(jax.random.fold_in(_tk, 500 + 13), (125000, 16), jnp.float32)
        tbl_14 = 0.05 * jax.random.normal(jax.random.fold_in(_tk, 500 + 14), (1250, 16), jnp.float32)
        tbl_15 = 0.05 * jax.random.normal(jax.random.fold_in(_tk, 500 + 15), (125000, 16), jnp.float32)
        tbl_16 = 0.05 * jax.random.normal(jax.random.fold_in(_tk, 500 + 16), (1250, 16), jnp.float32)
        tbl_17 = 0.05 * jax.random.normal(jax.random.fold_in(_tk, 500 + 17), (125000, 16), jnp.float32)
        tbl_18 = 0.05 * jax.random.normal(jax.random.fold_in(_tk, 500 + 18), (125000, 16), jnp.float32)
        tbl_19 = 0.05 * jax.random.normal(jax.random.fold_in(_tk, 500 + 19), (125000, 16), jnp.float32)
        tbl_20 = 0.05 * jax.random.normal(jax.random.fold_in(_tk, 500 + 20), (1000, 16), jnp.float32)
        tbl_21 = 0.05 * jax.random.normal(jax.random.fold_in(_tk, 500 + 21), (1000, 16), jnp.float32)
        tbl_22 = 0.05 * jax.random.normal(jax.random.fold_in(_tk, 500 + 22), (12500, 16), jnp.float32)
        tbl_23 = 0.05 * jax.random.normal(jax.random.fold_in(_tk, 500 + 23), (1000, 16), jnp.float32)
        tbl_24 = 0.05 * jax.random.normal(jax.random.fold_in(_tk, 500 + 24), (1250, 16), jnp.float32)
        tbl_25 = 0.05 * jax.random.normal(jax.random.fold_in(_tk, 500 + 25), (1250, 16), jnp.float32)
        tbl_26 = 0.05 * jax.random.normal(jax.random.fold_in(_tk, 500 + 26), (1000, 16), jnp.float32)
        tbl_27 = 0.05 * jax.random.normal(jax.random.fold_in(_tk, 500 + 27), (12500, 16), jnp.float32)
        tbl_28 = 0.05 * jax.random.normal(jax.random.fold_in(_tk, 500 + 28), (1000, 16), jnp.float32)
        tbl_29 = 0.05 * jax.random.normal(jax.random.fold_in(_tk, 500 + 29), (1000, 16), jnp.float32)
        tbl_30 = 0.05 * jax.random.normal(jax.random.fold_in(_tk, 500 + 30), (125000, 16), jnp.float32)
        tbl_31 = 0.05 * jax.random.normal(jax.random.fold_in(_tk, 500 + 31), (1250, 16), jnp.float32)
        _rk = jax.random.fold_in(_tk, 7)
        W_top1 = 0.0693375 * jax.random.normal(jax.random.fold_in(_tk, 801), (208, 512), jnp.float32)
        W_top2 = 0.0441942 * jax.random.normal(jax.random.fold_in(_tk, 802), (512, 256), jnp.float32)
        W_top3 = 0.0625 * jax.random.normal(jax.random.fold_in(_tk, 803), (256, 1), jnp.float32)
        b_top1 = jnp.zeros((512,), jnp.float32)
        b_top2 = jnp.zeros((256,), jnp.float32)
        return (dense_ctx, ids, tbl_0, tbl_1, tbl_2, tbl_3, tbl_4, tbl_5, tbl_6, tbl_7, tbl_8, tbl_9, tbl_10, tbl_11, tbl_12, tbl_13, tbl_14, tbl_15, tbl_16, tbl_17, tbl_18, tbl_19, tbl_20, tbl_21, tbl_22, tbl_23, tbl_24, tbl_25, tbl_26, tbl_27, tbl_28, tbl_29, tbl_30, tbl_31, W_top1, b_top1, W_top2, b_top2, W_top3)
    dense_ctx, ids, tbl_0, tbl_1, tbl_2, tbl_3, tbl_4, tbl_5, tbl_6, tbl_7, tbl_8, tbl_9, tbl_10, tbl_11, tbl_12, tbl_13, tbl_14, tbl_15, tbl_16, tbl_17, tbl_18, tbl_19, tbl_20, tbl_21, tbl_22, tbl_23, tbl_24, tbl_25, tbl_26, tbl_27, tbl_28, tbl_29, tbl_30, tbl_31, W_top1, b_top1, W_top2, b_top2, W_top3 = _rec_inputs()

    def _L0_rec_setup():
        import jax, jax.numpy as jnp
        import numpy as np
        B, M, D = (2048, 32, 16)
        LAYERS = [64, 64, 64]
        key = jax.random.key(seed)
        ks = jax.random.split(key, 4)
        inp = {'embeddings': jax.random.normal(ks[0], (B, M, D), dtype=jnp.float32)}
        hk_1 = M
        for i, hk in enumerate(LAYERS):
            scale = (2.0 / (M * hk_1 + hk)) ** 0.5
            inp[f'W{i}'] = jax.random.normal(ks[i + 1], (M, hk_1, hk), dtype=jnp.float32) * scale
            hk_1 = hk
        return inp
    _L0_rec_all = _L0_rec_setup()
    _L0_rec_in = {k: v for k, v in _L0_rec_all.items() if k in ('W0', 'W1', 'W2')}
    del _L0_rec_all
    return {'dense_ctx': dense_ctx, 'ids': ids, 'tbl_0': tbl_0, 'tbl_1': tbl_1, 'tbl_2': tbl_2, 'tbl_3': tbl_3, 'tbl_4': tbl_4, 'tbl_5': tbl_5, 'tbl_6': tbl_6, 'tbl_7': tbl_7, 'tbl_8': tbl_8, 'tbl_9': tbl_9, 'tbl_10': tbl_10, 'tbl_11': tbl_11, 'tbl_12': tbl_12, 'tbl_13': tbl_13, 'tbl_14': tbl_14, 'tbl_15': tbl_15, 'tbl_16': tbl_16, 'tbl_17': tbl_17, 'tbl_18': tbl_18, 'tbl_19': tbl_19, 'tbl_20': tbl_20, 'tbl_21': tbl_21, 'tbl_22': tbl_22, 'tbl_23': tbl_23, 'tbl_24': tbl_24, 'tbl_25': tbl_25, 'tbl_26': tbl_26, 'tbl_27': tbl_27, 'tbl_28': tbl_28, 'tbl_29': tbl_29, 'tbl_30': tbl_30, 'tbl_31': tbl_31, 'W_top1': W_top1, 'b_top1': b_top1, 'W_top2': W_top2, 'b_top2': b_top2, 'W_top3': W_top3, 'L0_rec_W0': _L0_rec_in['W0'], 'L0_rec_W1': _L0_rec_in['W1'], 'L0_rec_W2': _L0_rec_in['W2']}

def reference(dense_ctx, ids, tbl_0, tbl_1, tbl_2, tbl_3, tbl_4, tbl_5, tbl_6, tbl_7, tbl_8, tbl_9, tbl_10, tbl_11, tbl_12, tbl_13, tbl_14, tbl_15, tbl_16, tbl_17, tbl_18, tbl_19, tbl_20, tbl_21, tbl_22, tbl_23, tbl_24, tbl_25, tbl_26, tbl_27, tbl_28, tbl_29, tbl_30, tbl_31, W_top1, b_top1, W_top2, b_top2, W_top3, L0_rec_W0, L0_rec_W1, L0_rec_W2):
    import jax
    import jax.numpy as jnp

    def _L0_rec_ref(embeddings, W0, W1, W2):
        import jax, jax.numpy as jnp
        import numpy as np
        B, M, D = (2048, 32, 16)
        LAYERS = [64, 64, 64]
        x0 = embeddings
        xk = x0
        outs = []
        for W in (W0, W1, W2):
            xk = jax.nn.relu(jnp.einsum('bmd,bhd,mhk->bkd', x0, xk, W))
            outs.append(jnp.sum(xk, axis=2))
        return jnp.concatenate(outs, axis=1)
    e = jnp.stack([tbl_0[ids[:, 0]], tbl_1[ids[:, 1]], tbl_2[ids[:, 2]], tbl_3[ids[:, 3]], tbl_4[ids[:, 4]], tbl_5[ids[:, 5]], tbl_6[ids[:, 6]], tbl_7[ids[:, 7]], tbl_8[ids[:, 8]], tbl_9[ids[:, 9]], tbl_10[ids[:, 10]], tbl_11[ids[:, 11]], tbl_12[ids[:, 12]], tbl_13[ids[:, 13]], tbl_14[ids[:, 14]], tbl_15[ids[:, 15]], tbl_16[ids[:, 16]], tbl_17[ids[:, 17]], tbl_18[ids[:, 18]], tbl_19[ids[:, 19]], tbl_20[ids[:, 20]], tbl_21[ids[:, 21]], tbl_22[ids[:, 22]], tbl_23[ids[:, 23]], tbl_24[ids[:, 24]], tbl_25[ids[:, 25]], tbl_26[ids[:, 26]], tbl_27[ids[:, 27]], tbl_28[ids[:, 28]], tbl_29[ids[:, 29]], tbl_30[ids[:, 30]], tbl_31[ids[:, 31]]], axis=1)
    z = _L0_rec_ref(e, L0_rec_W0, L0_rec_W1, L0_rec_W2)
    z = z.reshape(z.shape[0], -1)
    h = jnp.concatenate([z, dense_ctx], axis=1)
    h = jnp.maximum(h @ W_top1 + b_top1, 0.0)
    h = jnp.maximum(h @ W_top2 + b_top2, 0.0)
    y = h @ W_top3
    return y

_drawn_inputs = setup_inputs


def setup_inputs(seed=0):
    import zlib

    import numpy as np

    out = dict(_drawn_inputs(seed))
    spreads = {'b_top1': (0.0, 2.0), 'b_top2': (0.0, 0.8)}
    factors = {'tbl_0': 8.0,
     'tbl_1': 8.0,
     'tbl_2': 8.0,
     'tbl_3': 8.0,
     'tbl_4': 8.0,
     'tbl_5': 8.0,
     'tbl_6': 8.0,
     'tbl_7': 8.0,
     'tbl_8': 8.0,
     'tbl_9': 8.0,
     'tbl_10': 8.0,
     'tbl_11': 8.0,
     'tbl_12': 8.0,
     'tbl_13': 8.0,
     'tbl_14': 8.0,
     'tbl_15': 8.0,
     'tbl_16': 8.0,
     'tbl_17': 8.0,
     'tbl_18': 8.0,
     'tbl_19': 8.0,
     'tbl_20': 8.0,
     'tbl_21': 8.0,
     'tbl_22': 8.0,
     'tbl_23': 8.0,
     'tbl_24': 8.0,
     'tbl_25': 8.0,
     'tbl_26': 8.0,
     'tbl_27': 8.0,
     'tbl_28': 8.0,
     'tbl_29': 8.0,
     'tbl_30': 8.0,
     'tbl_31': 8.0,
     'L0_rec_W0': 3.631,
     'L0_rec_W1': 8.0,
     'L0_rec_W2': 8.0,
     'dense_ctx': 7.422}
    for name, (base, spread) in spreads.items():
        noise = np.random.default_rng([zlib.crc32(name.encode()), seed]).standard_normal(out[name].shape)
        drawn = base * np.exp(spread * noise) if base else spread * noise
        out[name] = jnp.asarray(drawn.astype(out[name].dtype))
    for name, factor in factors.items():
        out[name] = (out[name] * factor).astype(out[name].dtype)
    return out
```

```python
from contextlib import ExitStack

import numpy as np
import concourse.bass as bass
from concourse import mybir

F32 = mybir.dt.float32
I32 = mybir.dt.int32
ALU = mybir.AluOpType
ACT = mybir.ActivationFunctionType

SUMS = 5
BATCH, FIELDS, DIM, HID = 1024, 32, 16, 64
P128 = 128
QUAD = 32
TILES = BATCH // P128
DPP = 4
PPT = DIM // DPP
PAIRS = TILES * PPT
COLS = DPP * P128
CHUNK = COLS // 2
ROT = P128 // FIELDS
L1_FULL = FIELDS // 2 // ROT
L1_TILES = L1_FULL + 1
WHEEL = FIELDS + FIELDS // 2
DVE_PAIRS = 3
MT = FIELDS // 4
GROUP = 4
GROUPS = 2 * MT // GROUP
TPC = FIELDS // PPT
TOP1, TOP2 = 512, 256
M1, M2 = TOP1 // P128, TOP2 // P128
HALF = BATCH // 2


def build_program(nc, dense_t, ids, tables, w0_fwd, w0_bwd, w1_cin, w2_cin,
                  w_top1, b_top1, w_top2, b_top2, w_top3, y_out):
    ctx = ExitStack()
    with ctx:
        def sb(name, shape, dt=F32):
            return ctx.enter_context(nc.sbuf_tensor(name, shape, dt))

        def pb(name, shape):
            return ctx.enter_context(nc.psum_tensor(name, shape, F32))

        def sem(name):
            return ctx.enter_context(nc.semaphore(name))

        ids_sb = sb("ids_sb", [P128, FIELDS], I32)
        rows = sb("rows", [P128, FIELDS, DIM])
        rows4 = sb("rows4", [P128, DIM, 4, FIELDS])
        ident = sb("ident", [P128, P128])
        x4 = sb("x4", [P128, 2, COLS])
        rot = sb("rot", [P128, 2, L1_TILES, COLS])
        z1 = sb("z1", [P128, 2, L1_TILES, COLS])
        xb = sb("xb", [P128, PPT, MT, COLS])
        z = sb("z", [P128, GROUPS, GROUP, COLS])
        r12 = sb("r12", [P128, PPT, COLS])
        r3 = sb("r3", [HID, PPT, COLS])
        r = [r12[0:HID, :, :], r12[HID:P128, :, :], r3[:, :, :]]
        zacc = [sb("zacc12", [P128, COLS]), sb("zacc3", [HID, COLS])]
        zsum = [sb("zsum12", [P128, BATCH]), sb("zsum3d", [HID + DIM, BATCH])]
        w0_sb = sb("w0_sb", [P128, L1_TILES, HID])
        w0b_sb = sb("w0b_sb", [P128, L1_FULL, HID])
        w1_sb = sb("w1_sb", [P128, 2 * MT, HID])
        w2_sb = sb("w2_sb", [P128, 2 * MT, HID])
        wt1_sb = sb("wt1_sb", [P128, 2, TOP1])
        wt2_sb = sb("wt2_sb", [P128, M1, TOP2])
        wt3_sb = sb("wt3_sb", [P128, M2])
        bt1_sb = sb("bt1_sb", [P128, M1])
        bt2_sb = sb("bt2_sb", [P128, M2])
        h1 = xb[:, 0, :, :].rearrange("p (h m) n -> p h m n", h=2)
        h2 = xb[:, 1, 0:2 * M2, :].rearrange("p (h m) n -> p h m n", h=2)
        y_sb = xb[0:1, 2, 0:2, :].rearrange("p h n -> p (h n)")

        wheel = nc.dram_tensor("wheel", (PPT, WHEEL, COLS), F32, kind="Internal").ap()

        xk = [pb(f"xk{n}", [P128, 2, COLS]) for n in (2, 3)]
        acc = [pb(f"acc{n}", [P128, COLS]) for n in range(2)]
        turned = pb("turned", [P128, COLS])
        tower = pb("tower", [P128, COLS])
        h1_ps = [xk[0][:, 0, :], xk[0][:, 1, :], xk[1][:, 0, :], xk[1][:, 1, :]]
        h2_ps = [acc[0][:, :], acc[1][:, :]]
        y_ps = [turned[0:1, :], tower[QUAD:QUAD + 1, :]]

        ids_loaded = [sem(f"ids_loaded{c}") for c in range(PPT)]
        gathered = [sem(f"gathered{c}") for c in range(PPT)]
        gather_let_go = sem("gather_let_go")
        ident_zero, ident_ready = sem("ident_zero"), sem("ident_ready")
        cin_w_loaded = [sem("w0_loaded"), sem("w1_loaded"), sem("w2_loaded")]
        w0_ready = sem("w0_ready")
        tower_loaded = sem("tower_loaded")
        rows_spread = sem("rows_spread")
        pair_turned = sem("pair_turned")
        x4_ready = sem("x4_ready")
        wheel_stored = [sem(f"wheel_stored{s}") for s in range(2)]
        rot_loaded = [sem(f"rot_loaded{s}") for s in range(2)]
        xb_loaded = [sem(f"xb_loaded{s}") for s in range(PPT)]
        z1_ready = sem("z1_ready")
        l1_done = sem("l1_done")
        z_ready = [sem("z2_ready"), sem("z3_ready")]
        z_used = [sem("z2_used"), sem("z3_used")]
        r_ready = [sem(f"r{n}_ready") for n in (1, 2, 3)]
        xk_ready = [sem("xk2_ready"), sem("xk3_ready")]
        summed = [sem("summed12"), sem("summed3")]
        h1_done, h1_ready = sem("h1_done"), sem("h1_ready")
        h2_done, h2_ready = sem("h2_done"), sem("h2_ready")
        y_done, y_ready, y_stored = sem("y_done"), sem("y_ready"), sem("y_stored")

        def wait(eng, s, value):
            if not isinstance(value, int) or value > 0:
                eng.wait_ge(s, value)

        def in_range(t):
            return not isinstance(t, int) or 0 <= t < PAIRS

        def steps(eng, step, last, first=0):
            for tile in range(first, 2):
                for j in range(PPT):
                    step(tile, j)
            with eng.Fori(2, last + 1) as tile:
                for j in range(PPT):
                    step(tile, j)
            for tile in range(last + 1, TILES + 2):
                for j in range(PPT):
                    step(tile, j)

        block = ctx.enter_context(nc.Block())

        @block.sync
        def _(sp):
            def load_ids(tile, c):
                sp.dma_start(ids_sb[:, TPC * c:TPC * (c + 1)],
                             ids[bass.ts(tile, P128), TPC * c:TPC * (c + 1)]).then_inc(ids_loaded[c], 16)

            for c in range(PPT):
                load_ids(0, c)
            sp.dma_start(w0_sb[:, 0:L1_FULL, :], w0_fwd[:, 0:L1_FULL, :]).then_inc(cin_w_loaded[0], 16)
            sp.dma_start(w0_sb[0:FIELDS, L1_FULL, :], w0_fwd[0:FIELDS, L1_FULL, :]).then_inc(cin_w_loaded[0], 16)
            sp.dma_start(w0b_sb[:, :, :], w0_bwd).then_inc(cin_w_loaded[0], 16)
            sp.dma_start(w1_sb[:, :, :], w1_cin).then_inc(cin_w_loaded[1], 16)
            sp.dma_start(w2_sb[:, :, :], w2_cin).then_inc(cin_w_loaded[2], 16)
            for dst, src in ((wt1_sb[:, 0, :], w_top1[0:P128, :]), (wt1_sb[0:HID + DIM, 1, :], w_top1[P128:, :]),
                             (wt2_sb[:, :, :], w_top2), (wt3_sb[:, :], w_top3), (bt1_sb[:, :], b_top1),
                             (bt2_sb[:, :], b_top2), (zsum[1][HID:HID + DIM, :], dense_t)):
                sp.dma_start(dst, src).then_inc(tower_loaded, 16)

            def spread_fields(t, jj):
                wait(sp, z_ready[1], GROUPS * (t - 4) + GROUPS)
                for q in range(4):
                    src = wheel[jj, q:, :]
                    src = bass.AP(src.tensor, src.offset, [[0, QUAD], [4 * COLS, MT], [1, COLS]])
                    sp.dma_start(xb[QUAD * q:QUAD * (q + 1), jj, :, :], src).then_inc(xb_loaded[jj], 16)

            def step(tile, j):
                t = PPT * tile + j
                slot = j % 2
                if in_range(t):
                    sp.wait_ge(x4_ready, t + 1)
                    sp.dma_start(wheel[j], x4[0:WHEEL, slot, :]).then_inc(wheel_stored[slot], 16)
                    sp.wait_ge(wheel_stored[slot], 16 * (2 * tile + j // 2 + 1))
                    for g in range(ROT):
                        tiles = L1_TILES if g == 0 else L1_FULL
                        src = wheel[j, g:, :]
                        src = bass.AP(src.tensor, src.offset, [[COLS, FIELDS], [ROT * COLS, tiles], [1, COLS]])
                        sp.dma_start(rot[FIELDS * g:FIELDS * (g + 1), slot, 0:tiles, :], src)\
                            .then_inc(rot_loaded[slot], 16)
                if in_range(t - 1):
                    spread_fields(t - 1, (j - 1) % PPT)
                c = (j + 2) % PPT
                nxt = tile + (1 if j < 2 else 2)
                if not isinstance(nxt, int) or nxt < TILES:
                    sp.wait_ge(gathered[c], 16 * TPC * nxt)
                    load_ids(nxt, c)

            for c in range(2):
                sp.wait_ge(gathered[c], 16 * TPC)
                load_ids(1, c)
            steps(sp, step, TILES - 3)
            sp.wait_ge(y_ready, 2)
            sp.dma_start(y_out, y_sb).then_inc(y_stored, 16)
            sp.wait_ge(y_stored, 16)

        @block.gpsimd
        def _(pool):
            def gather(tile, c):
                pool.wait_ge(ids_loaded[c], 16 * (tile + 1))
                wait(pool, rows_spread, PPT * tile)
                pool.sem_inc(gather_let_go, 1)
                for n in range(TPC * c, TPC * (c + 1)):
                    pool.indirect_dma_start(
                        out=rows[:, n, :], out_offset=None, in_=tables[n],
                        in_offset=bass.IndirectOffsetOnAxis(ap=ids_sb[:, n:n + 1], axis=0),
                    ).then_inc(gathered[c], 16)

            def dim_sum(n, tile, jj):
                if jj == 0:
                    return
                t = PPT * tile + jj
                out, zs = (r12, zsum[0]) if n == 0 else (r3, zsum[1][0:HID, :])
                pool.wait_ge(r_ready[n + 1], t + 1)
                wait(pool, summed[n], SUMS * tile + jj - 1)
                first = out[:, 0, :] if jj == 1 else zacc[n][:, :]
                pool.tensor_tensor(zacc[n][:, :], first, out[:, jj, :], ALU.add).then_inc(summed[n], 1)
                if jj == PPT - 1:
                    pool.wait_ge(summed[n], SUMS * tile + 3)
                    pool.tensor_tensor(zacc[n][:, 0:CHUNK], zacc[n][:, 0:CHUNK], zacc[n][:, CHUNK:COLS], ALU.add)\
                        .then_inc(summed[n], 1)
                    pool.wait_ge(summed[n], SUMS * tile + 4)
                    pool.tensor_tensor(zs[:, bass.ts(tile, P128)], zacc[n][:, 0:P128], zacc[n][:, P128:CHUNK], ALU.add)\
                        .then_inc(summed[n], 1)

            pool.memset(ident[:, :], 0.0).then_inc(ident_zero, 1)
            pool.wait_ge(ident_zero, 1)
            pool.affine_select(out=ident[:, :], in_=ident[:, :], compare_op=ALU.not_equal, fill=1.0, base=0,
                               pattern=[[-1, P128]], channel_multiplier=1).then_inc(ident_ready, 1)
            for c in range(PPT):
                gather(0, c)

            def step(tile, j):
                t = PPT * tile + j - 1
                if in_range(t) and not (isinstance(t, int) and t < DVE_PAIRS):
                    slot = (j - 1) % 2
                    if isinstance(t, int) and t == DVE_PAIRS:
                        pool.wait_ge(z1_ready, 2 * DVE_PAIRS)
                    pool.wait_ge(rot_loaded[slot], 16 * ROT * (2 * tile + (j - 1) // 2 + 1))
                    pool.wait_ge(x4_ready, t + 1)
                    wait(pool, l1_done, t - 1)
                    pool.tensor_tensor(z1[:, slot, 0:L1_FULL, :],
                                       x4[:, slot, :].unsqueeze(1).broadcast_to([P128, L1_FULL, COLS]),
                                       rot[:, slot, 0:L1_FULL, :], ALU.mult).then_inc(z1_ready, 1)
                    pool.tensor_tensor(z1[0:FIELDS, slot, L1_FULL, :], x4[0:FIELDS, slot, :],
                                       rot[0:FIELDS, slot, L1_FULL, :], ALU.mult).then_inc(z1_ready, 1)
                if not isinstance(tile, int) or tile + 1 < TILES:
                    gather(tile + 1, j)
                for n in range(2):
                    lag = 4 + n
                    i, jj = tile + (j - lag) // PPT, (j - lag) % PPT
                    if not isinstance(i, int) or 0 <= i < TILES:
                        dim_sum(n, i, jj)

            steps(pool, step, TILES - 2)

        @block.scalar
        def _(act):
            def spread_rows(tile):
                for c in range(PPT):
                    act.wait_ge(gathered[c], 16 * TPC * (tile + 1))
                wait(act, pair_turned, PPT * tile)
                for jj in range(PPT):
                    dims = slice(DPP * jj, DPP * (jj + 1))
                    src = rows[:, :, dims].rearrange("p m d -> p d m").unsqueeze(2).broadcast_to([P128, DPP, 4, FIELDS])
                    nc.scalar.activation(rows4[:, dims, :, :], src, ACT.Copy).then_inc(rows_spread, 1)

            def relu(n, tile, jj, done, done_at, bank):
                act.wait_ge(done, done_at)
                wait(act, summed[n // 2], SUMS * (tile - 1) + max(jj, 1))
                for c in range(2):
                    last = nc.scalar.activation(r[n][:, jj, CHUNK * c:CHUNK * (c + 1)],
                                                acc[bank][HID * c:HID * (c + 1), 0:CHUNK], ACT.Relu)
                last.then_inc(r_ready[n], 1)

            def spread(n, t, jj):
                act.wait_ge(r_ready[n], t + 1)
                wait(act, z_ready[n], GROUPS * t)
                for q in (0, 2):
                    last = nc.scalar.activation(xk[n][QUAD * q:QUAD * (q + 2), 0, :], r[n][:, jj, :], ACT.Copy)
                last.then_inc(xk_ready[n], 1)
                for q in range(4):
                    k0 = QUAD * ((q + 1) % 2)
                    last = nc.scalar.activation(xk[n][QUAD * q:QUAD * (q + 1), 1, :], r[n][k0:k0 + QUAD, jj, :], ACT.Copy)
                last.then_inc(xk_ready[n], 1)

            def to_sbuf(p, tile, j):
                slot = j % 2
                act.wait_ge(pair_turned, p + 1)
                wait(act, z1_ready, 2 * (p - 2) + 2)
                wait(act, xb_loaded[j], 16 * 4 * tile)
                nc.scalar.activation(x4[:, slot, :], turned[:, :], ACT.Copy).then_inc(x4_ready, 1)

            spread_rows(0)

            def step(tile, j):
                p = PPT * tile + j
                t = p - 2
                if in_range(t):
                    relu(0, tile + (j - 2) // PPT, (j - 2) % PPT, l1_done, t + 1, (3 * j) % 2)
                    if isinstance(t, int) and t == 2:
                        spread_rows(1)
                    spread(0, t, (j - 2) % PPT)
                t = p - 3
                if in_range(t):
                    relu(1, tile + (j - 3) // PPT, (j - 3) % PPT, z_used[0], GROUPS * (t + 1), (3 * j + 1) % 2)
                if in_range(p):
                    to_sbuf(p, tile, j)
                if in_range(t):
                    spread(1, t, (j - 3) % PPT)
                if j == PPT - 1 and (not isinstance(tile, int) or tile + 1 < TILES):
                    spread_rows(tile + 1)
                t = p - 4
                if in_range(t):
                    relu(2, tile - 1, j, z_used[1], GROUPS * (t + 1), (3 * j + 2) % 2)

            for p in range(3):
                to_sbuf(p, 0, p)
            relu(0, 0, 0, l1_done, 1, 0)
            spread(0, 0, 0)
            to_sbuf(3, 0, 3)
            relu(0, 0, 1, l1_done, 2, 1)
            spread(0, 1, 1)
            relu(1, 0, 0, z_used[0], GROUPS, 0)
            spread(1, 0, 0)
            steps(act, step, TILES - 2, first=1)

            act.wait_ge(tower_loaded, 16 * 7)
            for half in range(2):
                for m in range(M1):
                    act.wait_ge(h1_done, M1 * half + m + 1)
                    nc.scalar.activation(h1[:, half, m, :], h1_ps[m], ACT.Relu, bias=bt1_sb[:, m:m + 1])\
                        .then_inc(h1_ready, 1)
            for half in range(2):
                for m in range(M2):
                    act.wait_ge(h2_done, M2 * half + m + 1)
                    nc.scalar.activation(h2[:, half, m, :], h2_ps[m], ACT.Relu, bias=bt2_sb[:, m:m + 1])\
                        .then_inc(h2_ready, 1)
            for half in range(2):
                act.wait_ge(y_done, half + 1)
                nc.scalar.activation(y_sb[:, HALF * half:HALF * (half + 1)], y_ps[half], ACT.Copy).then_inc(y_ready, 1)

        @block.vector
        def _(dve):
            dve.wait_ge(cin_w_loaded[0], 48)
            for lo, hi, a in ((QUAD, 2 * QUAD, 0), (2 * QUAD, P128, 0), (0, P128, 1)):
                b = L1_FULL if a else 1
                nc.vector.tensor_tensor(w0_sb[lo:hi, a:b, :], w0_sb[lo:hi, a:b, :], w0b_sb[lo:hi, a:b, :],
                                        ALU.add).then_inc(w0_ready, 1)

            def products(n, t, s, tile_s):
                dve.wait_ge(xb_loaded[s], 16 * 4 * (tile_s + 1))
                for g in range(GROUPS):
                    u, v0 = g // 2, GROUP * (g % 2)
                    if g % 2 == 0:
                        dve.wait_ge(xk_ready[n], 2 * t + u + 1)
                    if n == 0 and isinstance(t, int) and t == 1:
                        dve.wait_ge(z_used[0], g + 1)
                    elif n == 0:
                        wait(dve, z_used[1], GROUPS * (t - 2) + g + 1)
                    elif not (isinstance(t, int) and t == PAIRS - 1):
                        dve.wait_ge(z_used[0], GROUPS * (t + 1) + g + 1)
                    else:
                        dve.wait_ge(z_used[1], GROUPS * (t - 1) + g + 1)
                    nc.vector.tensor_tensor(z[:, g, :, :], xb[:, s, v0:v0 + GROUP, :],
                                            xk[n][:, u, :].unsqueeze(1).broadcast_to([P128, GROUP, COLS]),
                                            ALU.mult).then_inc(z_ready[n], 1)

            def first_products(t, slot):
                dve.wait_ge(rot_loaded[slot], 16 * ROT * (t // 2 + 1))
                dve.wait_ge(x4_ready, t + 1)
                wait(dve, l1_done, t - 1)
                nc.vector.tensor_tensor(z1[:, slot, 0:L1_FULL, :],
                                        x4[:, slot, :].unsqueeze(1).broadcast_to([P128, L1_FULL, COLS]),
                                        rot[:, slot, 0:L1_FULL, :], ALU.mult).then_inc(z1_ready, 1)
                nc.vector.tensor_tensor(z1[0:FIELDS, slot, L1_FULL, :], x4[0:FIELDS, slot, :],
                                        rot[0:FIELDS, slot, L1_FULL, :], ALU.mult).then_inc(z1_ready, 1)

            def step(tile, j):
                t = PPT * tile + j - 3
                if in_range(t):
                    products(0, t, (j - 3) % PPT, tile + (j - 3) // PPT)
                t = PPT * tile + j - 4
                if in_range(t):
                    products(1, t, j, tile - 1)

            first_products(0, 0)
            first_products(1, 1)
            products(0, 0, 0, 0)
            first_products(2, 0)
            steps(dve, step, TILES - 1, first=1)

        @block.tensor
        def _(pe):
            pe.wait_ge(ident_ready, 1)

            def layer1(t, slot, bank):
                pe.wait_ge(z1_ready, 2 * t + 2)
                wait(pe, r_ready[1], t - 1)
                for k in range(L1_TILES):
                    rows_k = P128 if k < L1_FULL else FIELDS
                    for c in range(2):
                        last = nc.tensor.matmul(acc[bank][HID * c:HID * (c + 1), 0:CHUNK], w0_sb[0:rows_k, k, :],
                                                z1[0:rows_k, slot, k, CHUNK * c:CHUNK * (c + 1)],
                                                start=k == 0, stop=k == L1_TILES - 1)
                last.then_inc(l1_done, 1)

            def layer(n, t, w, bank):
                for g in range(GROUPS):
                    pe.wait_ge(z_ready[n], GROUPS * t + g + 1)
                    for v in range(GROUP):
                        k = GROUP * g + v
                        for c in range(2):
                            last = nc.tensor.matmul(acc[bank][HID * c:HID * (c + 1), 0:CHUNK], w[:, k, :],
                                                    z[:, g, v, CHUNK * c:CHUNK * (c + 1)],
                                                    start=k == 0, stop=k == 2 * MT - 1)
                    last.then_inc(z_used[n], 1)

            def turn(p, j):
                pe.wait_ge(rows_spread, p + 1)
                wait(pe, x4_ready, p)
                for d in range(DPP):
                    last = nc.tensor.transpose(turned[:, P128 * d:P128 * (d + 1)],
                                               rows4[:, DPP * j + d, :, :].rearrange("p g m -> p (g m)"), ident[:, :])
                last.then_inc(pair_turned, 1)

            def step(tile, j):
                p = PPT * tile + j
                t = p - 2
                if in_range(t):
                    layer1(t, j % 2, (3 * j) % 2)
                t = p - 3
                if in_range(t):
                    wait(pe, r_ready[2], t - 1)
                    layer(0, t, w1_sb, (3 * j + 1) % 2)
                if in_range(p):
                    turn(p, j)
                t = p - 4
                if in_range(t):
                    pe.wait_ge(r_ready[0], t + 3 if not isinstance(t, int) else min(t + 3, PAIRS))
                    if isinstance(t, int) and t == PAIRS - 1:
                        pe.wait_ge(r_ready[2], t)
                    layer(1, t, w2_sb, (3 * j + 2) % 2)

            for p in range(3):
                turn(p, p)
            pe.wait_ge(w0_ready, 3)
            layer1(0, 0, 0)
            turn(3, 3)
            layer1(1, 1, 1)
            pe.wait_ge(cin_w_loaded[1], 16)
            pe.wait_ge(cin_w_loaded[2], 16)
            layer(0, 0, w1_sb, 0)
            steps(pe, step, TILES - 1, first=1)

            pe.wait_ge(tower_loaded, 16 * 7)
            for half in range(2):
                cols = slice(HALF * half, HALF * (half + 1))
                for n in range(2):
                    pe.wait_ge(summed[n], SUMS * (TILES // 2) * (half + 1))
                for m in range(M1):
                    if half == 0:
                        pe.wait_ge(z_ready[m // 2], GROUPS * PAIRS)
                    else:
                        pe.wait_ge(h1_ready, m + 1)
                    ms = slice(P128 * m, P128 * (m + 1))
                    nc.tensor.matmul(h1_ps[m], wt1_sb[:, 0, ms], zsum[0][:, cols], start=True, stop=False)
                    nc.tensor.matmul(h1_ps[m], wt1_sb[0:HID + DIM, 1, ms], zsum[1][:, cols], start=False, stop=True)\
                        .then_inc(h1_done, 1)
            for half in range(2):
                for m in range(M2):
                    if half == 0:
                        pe.wait_ge(r_ready[2], PAIRS)
                    else:
                        pe.wait_ge(h2_ready, m + 1)
                    for k in range(M1):
                        pe.wait_ge(h1_ready, M1 * half + k + 1)
                        last = nc.tensor.matmul(h2_ps[m], wt2_sb[:, k, P128 * m:P128 * (m + 1)], h1[:, half, k, :],
                                                start=k == 0, stop=k == M1 - 1)
                    last.then_inc(h2_done, 1)
            pe.wait_ge(x4_ready, PAIRS)
            for k in range(M2):
                for half in range(2):
                    pe.wait_ge(h2_ready, M2 * half + k + 1)
                    last = nc.tensor.matmul(y_ps[half], wt3_sb[:, k:k + 1], h2[:, half, k, :], start=k == 0, stop=k == M2 - 1)
                    if k == M2 - 1:
                        last.then_inc(y_done, 1)


def rotated(w):
    m = np.arange(FIELDS)[None, :, None]
    s = np.arange(ROT)[:, None, None] + ROT * np.arange(L1_TILES)[None, None, :]
    other = (m + s) % FIELDS
    fwd = w[m, other].reshape(P128, L1_TILES, HID)
    bwd = w[other, m].reshape(P128, L1_TILES, HID)[:, :L1_FULL]
    return np.ascontiguousarray(fwd), np.ascontiguousarray(bwd)


def interleaved(w):
    q = np.arange(4)[:, None, None, None]
    hh = np.arange(QUAD)[None, :, None, None]
    u = np.arange(2)[None, None, :, None]
    v = np.arange(MT)[None, None, None, :]
    out = w[4 * v + q, QUAD * ((q + u) % 2) + hh]
    return np.ascontiguousarray(out.reshape(P128, 2 * MT, HID))


def kernel(**inputs):
    import concourse.bacc as bacc
    from concourse.bass_utils import run_bass_kernel_spmd

    a = {k: np.asarray(v) for k, v in inputs.items()}
    w0_fwd, w0_bwd = rotated(a["L0_rec_W0"])
    arrays = {
        "dense_t": np.ascontiguousarray(a["dense_ctx"].T),
        "ids": a["ids"],
        "w0_fwd": w0_fwd, "w0_bwd": w0_bwd,
        "w1_cin": interleaved(a["L0_rec_W1"]), "w2_cin": interleaved(a["L0_rec_W2"]),
        "w_top1": a["W_top1"],
        "b_top1": np.ascontiguousarray(a["b_top1"].reshape(M1, P128).T),
        "w_top2": np.ascontiguousarray(a["W_top2"].reshape(M1, P128, TOP2).transpose(1, 0, 2)),
        "b_top2": np.ascontiguousarray(a["b_top2"].reshape(M2, P128).T),
        "w_top3": np.ascontiguousarray(a["W_top3"].reshape(M2, P128).T),
    }
    for n in range(FIELDS):
        arrays[f"tbl_{n}"] = a[f"tbl_{n}"]
    nc = bacc.Bacc("TRN2", target_bir_lowering=False, num_devices=1)
    aps = {k: nc.dram_tensor(k, v.shape, mybir.dt.from_np(v.dtype), kind="ExternalInput").ap()
           for k, v in arrays.items()}
    y = nc.dram_tensor("y", (1, BATCH), F32, kind="ExternalOutput").ap()
    build_program(nc, aps["dense_t"], aps["ids"], [aps[f"tbl_{n}"] for n in range(FIELDS)],
                  aps["w0_fwd"], aps["w0_bwd"], aps["w1_cin"], aps["w2_cin"], aps["w_top1"],
                  aps["b_top1"], aps["w_top2"], aps["b_top2"], aps["w_top3"], y)
    result = run_bass_kernel_spmd(nc, [arrays], core_ids=[0])
    return result.results[0]["y"].reshape(BATCH, 1)
```

```python
from contextlib import ExitStack

import numpy as np
import concourse.bass as bass
from concourse import mybir

F32 = mybir.dt.float32
I32 = mybir.dt.int32
ALU = mybir.AluOpType
ACT = mybir.ActivationFunctionType

SUMS = 5
BATCH, FIELDS, DIM, HID = 1024, 32, 16, 64
P128 = 128
QUAD = 32
TILES = BATCH // P128
DPP = 4
PPT = DIM // DPP
PAIRS = TILES * PPT
COLS = DPP * P128
CHUNK = COLS // 2
ROT = P128 // FIELDS
L1_FULL = FIELDS // 2 // ROT
L1_TILES = L1_FULL + 1
WHEEL = FIELDS + FIELDS // 2
DVE_PAIRS = 3
MT = FIELDS // 4
GROUP = 4
GROUPS = 2 * MT // GROUP
TPC = FIELDS // PPT
TOP1, TOP2 = 512, 256
M1, M2 = TOP1 // P128, TOP2 // P128
PICKED = 12
SPREAD = 125
HALF = BATCH // 2


def small_tables(sizes):
    return sorted((n for n in range(FIELDS) if sizes[n] <= 10 * SPREAD and sizes[n] % SPREAD == 0),
                  key=lambda n: sizes[n])[:PICKED]


def build_program(nc, dense_t, ids, ids_picked, tables, w0_fwd, w0_bwd, w1_cin, w2_cin,
                  w_top1, b_top1, w_top2, b_top2, w_top3, y_out):
    ctx = ExitStack()
    with ctx:
        def sb(name, shape, dt=F32):
            return ctx.enter_context(nc.sbuf_tensor(name, shape, dt))

        def pb(name, shape):
            return ctx.enter_context(nc.psum_tensor(name, shape, F32))

        def sem(name):
            return ctx.enter_context(nc.semaphore(name))

        ids_sb = sb("ids_sb", [P128, FIELDS], I32)
        rows = sb("rows", [P128, FIELDS, DIM])
        ids0_sb = sb("ids0_sb", [P128, FIELDS], I32)
        rows0 = sb("rows0", [P128, FIELDS, DIM])
        ids_wide = sb("ids_wide", [SPREAD, PICKED, P128], I32)
        rows4 = sb("rows4", [P128, DIM, 4, FIELDS])
        ident = sb("ident", [P128, P128])
        x4 = sb("x4", [P128, 2, COLS])
        rot = sb("rot", [P128, 2, L1_TILES, COLS])
        z1 = sb("z1", [P128, 2, L1_TILES, COLS])
        xb = sb("xb", [P128, PPT, MT, COLS])
        z = sb("z", [P128, 2, 2, GROUP, COLS])
        r12 = sb("r12", [P128, PPT, COLS])
        r3 = sb("r3", [HID, PPT, COLS])
        r = [r12[0:HID, :, :], r12[HID:P128, :, :], r3[:, :, :]]
        zacc = [sb("zacc12", [P128, COLS]), sb("zacc3", [HID, COLS])]
        zsum = [sb("zsum12", [P128, BATCH]), sb("zsum3d", [HID + DIM, BATCH])]
        w0_sb = sb("w0_sb", [P128, L1_TILES, HID])
        w0b_sb = sb("w0b_sb", [P128, L1_FULL, HID])
        w1_sb = sb("w1_sb", [P128, 2 * MT, HID])
        w2_sb = sb("w2_sb", [P128, 2 * MT, HID])
        wt1_sb = sb("wt1_sb", [P128, 2, TOP1])
        wt2_sb = sb("wt2_sb", [P128, M1, TOP2])
        wt3_sb = sb("wt3_sb", [P128, M2])
        bt1_sb = sb("bt1_sb", [P128, M1])
        bt2_sb = sb("bt2_sb", [P128, M2])
        picked = small_tables([t.shape[0] for t in tables])
        chunks = [tables[n].shape[0] // SPREAD for n in picked]
        held = xb[0:SPREAD, 3, 0:4, :].rearrange("p v n -> p (v n)")
        ids_f = xb[0:SPREAD, 2, 0:PICKED // 4, :].rearrange("p v (i n) -> p (v i) n", n=P128)
        row_no = {c: xb[0:SPREAD, 1, 6 + k, 0:c] for k, c in enumerate(sorted(set(chunks)))}
        flat = [xb[0:SPREAD, 0:2, :, :].rearrange("p s v n -> p (s v n)"),
                z[0:SPREAD, :, :, :, :].rearrange("p l s g n -> p (l s g n)")]
        one_hot = []
        for i, c in enumerate(chunks):
            at = max(chunks) * P128 * (i % 4)
            one_hot.append(flat[i // 4 % 2][:, at:at + c * P128])
        picked_t = rot[:, 0, 0:2, 0:P128]
        rot0_rows = z[:, 1, :, :, :].rearrange("p s g n -> p (s g n)")[:, 0:DPP * FIELDS * (FIELDS // 2 + 1)]\
            .rearrange("p (d w) -> p d w", d=DPP)
        h1 = xb[:, 0, :, :].rearrange("p (h m) n -> p h m n", h=2)
        h2 = xb[:, 1, 0:2 * M2, :].rearrange("p (h m) n -> p h m n", h=2)
        y_sb = xb[0:1, 2, 0:2, :].rearrange("p h n -> p (h n)")

        wheel = nc.dram_tensor("wheel", (PPT, WHEEL, COLS), F32, kind="Internal").ap()

        xk = [pb(f"xk{n}", [P128, 2, COLS]) for n in (2, 3)]
        acc1 = pb("acc_l1", [P128, COLS])
        acc = [pb(f"acc_l23_{n}", [P128, COLS]) for n in range(2)]
        turned = pb("turned", [P128, COLS])
        rot0_ps = [xk[0][:, 0, :], xk[0][:, 1, :], xk[1][:, 0, :], xk[1][:, 1, :], acc[0][0:FIELDS, :]]
        h1_ps = [xk[0][:, 0, :], xk[0][:, 1, :], xk[1][:, 0, :], xk[1][:, 1, :]]
        h2_ps = [acc[0][:, :], acc[1][:, :]]
        y_ps = [turned[0:1, :], acc1[QUAD:QUAD + 1, :]]

        ids_loaded = [sem(f"ids_loaded{c}") for c in range(PPT)]
        gathered = [sem(f"gathered{c}") for c in range(PPT)]
        gather_let_go = sem("gather_let_go")
        ids0_loaded, wide_loaded = sem("ids0_loaded"), sem("wide_loaded")
        tables_loaded = sem("tables_loaded")
        gathered0 = sem("gathered0_rows")
        row_no_ready = sem("row_no_ready")
        ids_f_ready = sem("ids_f_ready")
        one_hot_ready = sem("one_hot_ready")
        picked_done = sem("picked_done")
        picked_t_clear = sem("picked_t_clear")
        picked_t_ready = sem("picked_t_ready")
        picked_turned = sem("picked_turned")
        picked_stored = sem("picked_stored")
        ident_zero, ident_ready = sem("ident_zero"), sem("ident_ready")
        cin_w_loaded = [sem("w0_loaded"), sem("w1_loaded"), sem("w2_loaded")]
        w0_ready = sem("w0_ready")
        tower_loaded = sem("tower_loaded")
        rows_spread = sem("rows_spread")
        pair_turned = sem("pair_turned")
        rot0_spread = sem("rot0_spread")
        rot0_turned = sem("rot0_turned")
        x4_ready = sem("x4_ready")
        wheel_stored = [sem(f"wheel_stored{s}") for s in range(2)]
        rot_loaded = [sem(f"rot_loaded{s}") for s in range(2)]
        xb_loaded = [sem(f"xb_loaded{s}") for s in range(PPT)]
        z1_ready = sem("z1_ready")
        l1_done = sem("l1_done")
        z_ready = [sem("z2_ready"), sem("z3_ready")]
        z_used = [sem("z2_used"), sem("z3_used")]
        r_ready = [sem(f"r{n}_ready") for n in (1, 2, 3)]
        xk_ready = [sem("xk2_ready"), sem("xk3_ready")]
        summed = [sem("summed12"), sem("summed3")]
        h1_done, h1_ready = sem("h1_done"), sem("h1_ready")
        h2_done, h2_ready = sem("h2_done"), sem("h2_ready")
        y_done, y_ready, y_stored = sem("y_done"), sem("y_ready"), sem("y_stored")

        def wait(eng, s, value):
            if not isinstance(value, int) or value > 0:
                eng.wait_ge(s, value)

        def in_range(t):
            return not isinstance(t, int) or 0 <= t < PAIRS

        def alone(p):
            return in_range(p - 3) != in_range(p - 5)

        def steps(eng, step, last, first=0, peeled=2):
            for tile in range(first, peeled):
                for j in range(PPT):
                    step(tile, j)
            with eng.Fori(peeled, last + 1) as tile:
                for j in range(PPT):
                    step(tile, j)
            for tile in range(last + 1, TILES + 2):
                for j in range(PPT):
                    step(tile, j)

        block = ctx.enter_context(nc.Block())

        @block.sync
        def _(sp):
            def load_ids(tile, c):
                sp.dma_start(ids_sb[:, TPC * c:TPC * (c + 1)],
                             ids[bass.ts(tile, P128), TPC * c:TPC * (c + 1)]).then_inc(ids_loaded[c], 16)

            sp.dma_start(ids0_sb[:, :], ids[0:P128, :]).then_inc(ids0_loaded, 16)
            sp.dma_start(ids_wide[:, :, :],
                         bass.AP(ids_picked.tensor, 0, [[0, SPREAD], [P128, PICKED], [1, P128]])).then_inc(wide_loaded, 16)
            at = 0
            for n, c in zip(picked, chunks):
                sp.dma_start(held[:, at:at + c * DIM], tables[n].rearrange("(p c) d -> p (c d)", p=SPREAD))\
                    .then_inc(tables_loaded, 16)
                at += c * DIM
            for c in range(PPT):
                load_ids(1, c)
            sp.dma_start(w0_sb[:, 0:L1_FULL, :], w0_fwd[:, 0:L1_FULL, :]).then_inc(cin_w_loaded[0], 16)
            sp.dma_start(w0_sb[0:FIELDS, L1_FULL, :], w0_fwd[0:FIELDS, L1_FULL, :]).then_inc(cin_w_loaded[0], 16)
            sp.dma_start(w0b_sb[:, :, :], w0_bwd).then_inc(cin_w_loaded[0], 16)
            sp.dma_start(w1_sb[:, :, :], w1_cin).then_inc(cin_w_loaded[1], 16)
            sp.dma_start(w2_sb[:, :, :], w2_cin).then_inc(cin_w_loaded[2], 16)
            for dst, src in ((wt1_sb[:, 0, :], w_top1[0:P128, :]), (wt1_sb[0:HID + DIM, 1, :], w_top1[P128:, :]),
                             (wt2_sb[:, :, :], w_top2), (wt3_sb[:, :], w_top3), (bt1_sb[:, :], b_top1),
                             (bt2_sb[:, :], b_top2), (zsum[1][HID:HID + DIM, :], dense_t)):
                sp.dma_start(dst, src).then_inc(tower_loaded, 16)

            def spread_fields(t, jj):
                wait(sp, z_ready[1], GROUPS * (t - 4) + GROUPS)
                for q in range(4):
                    src = wheel[jj, q:, :]
                    src = bass.AP(src.tensor, src.offset, [[0, QUAD], [4 * COLS, MT], [1, COLS]])
                    sp.dma_start(xb[QUAD * q:QUAD * (q + 1), jj, :, :], src).then_inc(xb_loaded[jj], 16)

            def step(tile, j):
                t = PPT * tile + j
                slot = j % 2
                if in_range(t - 2) and not (isinstance(t, int) and t < PPT + 2):
                    spread_fields(t - 2, (j - 2) % PPT)
                if in_range(t):
                    sp.wait_ge(x4_ready, t + 1)
                    sp.dma_start(wheel[j], x4[0:WHEEL, slot, :]).then_inc(wheel_stored[slot], 16)
                    sp.wait_ge(wheel_stored[slot], 16 * (2 * tile + j // 2 + 1))
                    for g in range(ROT if not isinstance(t, int) or t > 0 else 0):
                        tiles = L1_TILES if g == 0 else L1_FULL
                        src = wheel[j, g:, :]
                        src = bass.AP(src.tensor, src.offset, [[COLS, FIELDS], [ROT * COLS, tiles], [1, COLS]])
                        sp.dma_start(rot[FIELDS * g:FIELDS * (g + 1), slot, 0:tiles, :], src)\
                            .then_inc(rot_loaded[slot], 16)
                if isinstance(t, int) and t < PPT:
                    spread_fields(t, j)
                c = (j + 2) % PPT
                nxt = tile + (1 if j < 2 else 2)
                if not isinstance(nxt, int) or 2 <= nxt < TILES:
                    sp.wait_ge(gathered[c], 16 * TPC * (nxt - 1))
                    load_ids(nxt, c)

            steps(sp, step, TILES - 3)
            sp.wait_ge(y_ready, 2)
            sp.dma_start(y_out, y_sb).then_inc(y_stored, 16)
            sp.wait_ge(y_stored, 16)

        @block.gpsimd
        def _(pool):
            def gather(tile, c):
                pool.wait_ge(ids_loaded[c], 16 * tile)
                if not isinstance(tile, int) or tile > 1:
                    pool.wait_ge(rows_spread, PPT * tile)
                pool.sem_inc(gather_let_go, 1)
                for n in range(TPC * c, TPC * (c + 1)):
                    pool.indirect_dma_start(
                        out=rows[:, n, :], out_offset=None, in_=tables[n],
                        in_offset=bass.IndirectOffsetOnAxis(ap=ids_sb[:, n:n + 1], axis=0),
                    ).then_inc(gathered[c], 16)

            def dim_sum(n, tile, jj):
                if jj == 0:
                    return
                t = PPT * tile + jj
                out, zs = (r12, zsum[0]) if n == 0 else (r3, zsum[1][0:HID, :])
                pool.wait_ge(r_ready[n + 1], t + 1)
                wait(pool, summed[n], SUMS * tile + jj - 1)
                first = out[:, 0, :] if jj == 1 else zacc[n][:, :]
                pool.tensor_tensor(zacc[n][:, :], first, out[:, jj, :], ALU.add).then_inc(summed[n], 1)
                if jj == PPT - 1:
                    pool.wait_ge(summed[n], SUMS * tile + 3)
                    pool.tensor_tensor(zacc[n][:, 0:CHUNK], zacc[n][:, 0:CHUNK], zacc[n][:, CHUNK:COLS], ALU.add)\
                        .then_inc(summed[n], 1)
                    pool.wait_ge(summed[n], SUMS * tile + 4)
                    pool.tensor_tensor(zs[:, bass.ts(tile, P128)], zacc[n][:, 0:P128], zacc[n][:, P128:CHUNK], ALU.add)\
                        .then_inc(summed[n], 1)

            for c, numbers in row_no.items():
                pool.iota(numbers, pattern=[[1, c]], base=0, channel_multiplier=c,
                          allow_small_or_imprecise_dtypes=True).then_inc(row_no_ready, 1)
            pool.memset(picked_t, 0.0).then_inc(picked_t_clear, 1)
            pool.memset(ident[:, :], 0.0).then_inc(ident_zero, 1)
            pool.wait_ge(ident_zero, 1)
            pool.affine_select(out=ident[:, :], in_=ident[:, :], compare_op=ALU.not_equal, fill=1.0, base=0,
                               pattern=[[-1, P128]], channel_multiplier=1).then_inc(ident_ready, 1)
            pool.wait_ge(ids0_loaded, 16)
            for n in range(FIELDS):
                if n not in picked:
                    pool.indirect_dma_start(
                        out=rows0[:, n, :], out_offset=None, in_=tables[n],
                        in_offset=bass.IndirectOffsetOnAxis(ap=ids0_sb[:, n:n + 1], axis=0),
                    ).then_inc(gathered0, 16)

            def step(tile, j):
                t = PPT * tile + j - 1
                if in_range(t) and not (isinstance(t, int) and t < DVE_PAIRS):
                    slot = (j - 1) % 2
                    if isinstance(t, int) and t == DVE_PAIRS:
                        pool.wait_ge(z1_ready, 2 * DVE_PAIRS)
                    pool.wait_ge(rot_loaded[slot], 16 * ROT * (2 * tile + (j - 1) // 2 + slot))
                    pool.wait_ge(x4_ready, t + 1)
                    wait(pool, l1_done, t - 1)
                    pool.tensor_tensor(z1[:, slot, 0:L1_FULL, :],
                                       x4[:, slot, :].unsqueeze(1).broadcast_to([P128, L1_FULL, COLS]),
                                       rot[:, slot, 0:L1_FULL, :], ALU.mult).then_inc(z1_ready, 1)
                    pool.tensor_tensor(z1[0:FIELDS, slot, L1_FULL, :], x4[0:FIELDS, slot, :],
                                       rot[0:FIELDS, slot, L1_FULL, :], ALU.mult).then_inc(z1_ready, 1)
                if not isinstance(tile, int) or tile + 1 < TILES:
                    gather(tile + 1, j)
                for n in range(2):
                    lag = 4 + 2 * n
                    i, jj = tile + (j - lag) // PPT, (j - lag) % PPT
                    if not isinstance(i, int) or 0 <= i < TILES:
                        dim_sum(n, i, jj)

            steps(pool, step, TILES - 2)

        @block.scalar
        def _(act):
            def spread_rows(tile, pairs=range(PPT)):
                first = isinstance(tile, int) and tile == 0
                if first:
                    act.wait_ge(gathered0, 16 * (FIELDS - PICKED))
                    act.wait_ge(picked_stored, PICKED // 4)
                else:
                    for c in range(PPT):
                        act.wait_ge(gathered[c], 16 * TPC * tile)
                    act.wait_ge(pair_turned, PPT * tile)
                for jj in pairs:
                    dims = slice(DPP * jj, DPP * (jj + 1))
                    src = (rows0 if first else rows)[:, :, dims].rearrange("p m d -> p d m").unsqueeze(2).broadcast_to([P128, DPP, 4, FIELDS])
                    nc.scalar.activation(rows4[:, dims, :, :], src, ACT.Copy).then_inc(rows_spread, 1)

            def relu(n, tile, jj, done, done_at, sums, halves):
                act.wait_ge(done, done_at)
                wait(act, summed[n // 2], SUMS * (tile - 1) + max(jj, 1))
                if halves:
                    for c in range(2):
                        last = nc.scalar.activation(r[n][:, jj, CHUNK * c:CHUNK * (c + 1)],
                                                    sums[HID * c:HID * (c + 1), 0:CHUNK], ACT.Relu)
                else:
                    side = HID * (n - 1)
                    last = nc.scalar.activation(r[n][:, jj, :], sums[side:side + HID, :], ACT.Relu)
                last.then_inc(r_ready[n], 1)

            def spread(n, t, jj, u):
                act.wait_ge(r_ready[n], t + 1)
                wait(act, z_ready[n], GROUPS * (t - 1) + GROUPS // 2 * (u + 1))
                if u == 0:
                    for q in (0, 2):
                        last = nc.scalar.activation(xk[n][QUAD * q:QUAD * (q + 2), 0, :], r[n][:, jj, :], ACT.Copy)
                else:
                    for q in range(4):
                        k0 = QUAD * ((q + 1) % 2)
                        last = nc.scalar.activation(xk[n][QUAD * q:QUAD * (q + 1), 1, :], r[n][k0:k0 + QUAD, jj, :],
                                                    ACT.Copy)
                last.then_inc(xk_ready[n], 1)

            def to_sbuf(p, tile, j):
                slot = j % 2
                act.wait_ge(pair_turned, p + 1)
                wait(act, z1_ready, 2 * (p - 2) + 2)
                wait(act, xb_loaded[j], 16 * 4 * tile)
                nc.scalar.activation(x4[:, slot, :], turned[:, :], ACT.Copy).then_inc(x4_ready, 1)

            nc.scalar.preload_act_table(ACT.Relu)

            def step(tile, j):
                p = PPT * tile + j
                t1, t2 = p - 2, p - 4
                if in_range(t1):
                    relu(0, tile + (j - 2) // PPT, (j - 2) % PPT, l1_done, t1 + 1, acc1, True)
                    if isinstance(t1, int) and t1 == 2:
                        spread_rows(1)
                    spread(0, t1, (j - 2) % PPT, 0)
                if in_range(t2):
                    spread(1, t2, j, 0)
                if in_range(p):
                    to_sbuf(p, tile, j)
                if in_range(t1):
                    spread(0, t1, (j - 2) % PPT, 1)
                if in_range(t2):
                    spread(1, t2, j, 1)
                if j == PPT - 1 and (not isinstance(tile, int) or tile + 1 < TILES):
                    spread_rows(tile + 1)
                t = p - 3
                if in_range(t):
                    relu(1, tile + (j - 3) // PPT, (j - 3) % PPT, z_used[0], GROUPS * (t + 1), acc[j % 2], alone(p))
                t = p - 5
                if in_range(t):
                    relu(2, tile + (j - 5) // PPT, (j - 5) % PPT, z_used[1], GROUPS * (t + 1), acc[j % 2], alone(p))

            def store_picked(g):
                act.wait_ge(picked_turned, g + 1)
                for i in range(4):
                    last = nc.scalar.activation(rows0[:, picked[4 * g + i], :], turned[:, QUAD * i:QUAD * i + DIM], ACT.Copy)
                last.then_inc(picked_stored, 1)

            act.wait_ge(picked_t_clear, 1)
            for g in range(PICKED // 4):
                act.wait_ge(picked_done, g + 1)
                for i in range(4):
                    part = slice(QUAD * i, QUAD * i + DIM)
                    last = nc.scalar.activation(picked_t[part, g % 2, :], acc[g % 2][part, 0:P128], ACT.Copy)
                last.then_inc(picked_t_ready, 1)
                store_picked(g)
            spread_rows(0, range(2))
            to_sbuf(0, 0, 0)
            spread_rows(0, range(2, PPT))
            to_sbuf(1, 0, 1)
            act.wait_ge(wheel_stored[0], 16)
            to_sbuf(2, 0, 2)
            relu(0, 0, 0, l1_done, 1, acc1, True)
            spread(0, 0, 0, 0)
            spread(0, 0, 0, 1)
            to_sbuf(3, 0, 3)
            relu(0, 0, 1, l1_done, 2, acc1, True)
            spread(0, 1, 1, 0)
            spread(0, 1, 1, 1)
            relu(1, 0, 0, z_used[0], GROUPS, acc[1], True)
            steps(act, step, TILES - 2, first=1, peeled=3)

            act.wait_ge(tower_loaded, 16 * 7)
            for half in range(2):
                for m in range(M1):
                    act.wait_ge(h1_done, M1 * half + m + 1)
                    nc.scalar.activation(h1[:, half, m, :], h1_ps[m], ACT.Relu, bias=bt1_sb[:, m:m + 1])\
                        .then_inc(h1_ready, 1)
            for half in range(2):
                for m in range(M2):
                    act.wait_ge(h2_done, M2 * half + m + 1)
                    nc.scalar.activation(h2[:, half, m, :], h2_ps[m], ACT.Relu, bias=bt2_sb[:, m:m + 1])\
                        .then_inc(h2_ready, 1)
            for half in range(2):
                act.wait_ge(y_done, half + 1)
                nc.scalar.activation(y_sb[:, HALF * half:HALF * (half + 1)], y_ps[half], ACT.Copy).then_inc(y_ready, 1)

        @block.vector
        def _(dve):
            dve.wait_ge(wide_loaded, 16)
            nc.vector.tensor_copy(ids_f, ids_wide[:, :, :]).then_inc(ids_f_ready, 1)
            dve.wait_ge(ids_f_ready, 1)
            dve.wait_ge(row_no_ready, len(row_no))
            for i, c in enumerate(chunks):
                wait(dve, picked_done, i // 4 - 1)
                nc.vector.tensor_tensor(one_hot[i].rearrange("p (c n) -> p c n", c=c),
                                        ids_f[:, i, :].unsqueeze(1).broadcast_to([SPREAD, c, P128]),
                                        row_no[c].unsqueeze(2).broadcast_to([SPREAD, c, P128]),
                                        ALU.is_equal).then_inc(one_hot_ready, 1)
            dve.wait_ge(cin_w_loaded[0], 48)
            for lo, hi, a in ((QUAD, 2 * QUAD, 0), (2 * QUAD, P128, 0), (0, P128, 1)):
                b = L1_FULL if a else 1
                nc.vector.tensor_tensor(w0_sb[lo:hi, a:b, :], w0_sb[lo:hi, a:b, :], w0b_sb[lo:hi, a:b, :],
                                        ALU.add).then_inc(w0_ready, 1)

            def products(n, t, s, tile_s, g):
                u, v0 = g // 2, GROUP * (g % 2)
                if g == 0:
                    dve.wait_ge(xb_loaded[s], 16 * 4 * (tile_s + 1))
                if g % 2 == 0:
                    dve.wait_ge(xk_ready[n], 2 * t + u + 1)
                wait(dve, z_used[n], GROUPS * t + g - 1)
                nc.vector.tensor_tensor(z[:, n, g % 2, :, :], xb[:, s, v0:v0 + GROUP, :],
                                        xk[n][:, u, :].unsqueeze(1).broadcast_to([P128, GROUP, COLS]),
                                        ALU.mult).then_inc(z_ready[n], 1)

            def first_products(t, slot):
                dve.wait_ge(rot_loaded[slot], 16 * ROT * (t // 2 + slot))
                dve.wait_ge(x4_ready, t + 1)
                wait(dve, l1_done, t - 1)
                nc.vector.tensor_tensor(z1[:, slot, 0:L1_FULL, :],
                                        x4[:, slot, :].unsqueeze(1).broadcast_to([P128, L1_FULL, COLS]),
                                        rot[:, slot, 0:L1_FULL, :], ALU.mult).then_inc(z1_ready, 1)
                nc.vector.tensor_tensor(z1[0:FIELDS, slot, L1_FULL, :], x4[0:FIELDS, slot, :],
                                        rot[0:FIELDS, slot, L1_FULL, :], ALU.mult).then_inc(z1_ready, 1)

            def step(tile, j):
                for g in range(GROUPS):
                    for n, lag in ((0, 3), (1, 5)):
                        t = PPT * tile + j - lag
                        if in_range(t):
                            products(n, t, (j - lag) % PPT, tile + (j - lag) // PPT, g)
                    if isinstance(tile, int) and PPT * tile + j == PPT and g == 1:
                        first_products(2, 0)

            dve.wait_ge(rows_spread, 1)
            for s0, s1 in ((0, 2 * ROT), (2 * ROT, FIELDS // 2 + 1)):
                src = rows4[:, 0:DPP, 0, s0:]
                src = bass.AP(src.tensor, src.offset, [list(src.ap[0]), list(src.ap[1]), [1, s1 - s0], [1, FIELDS]])
                nc.vector.tensor_copy(rot0_rows[:, :, FIELDS * s0:FIELDS * s1].rearrange("p d (s m) -> p d s m", m=FIELDS),
                                      src).then_inc(rot0_spread, 1)
            dve.wait_ge(x4_ready, 1)
            for n in range(2):
                dve.wait_ge(rot0_turned, n + 1)
                last = nc.vector.tensor_tensor(z1[:, 0, 2 * n:2 * n + 2, :],
                                               x4[:, 0, :].unsqueeze(1).broadcast_to([P128, 2, COLS]),
                                               xk[n][:, :, :], ALU.mult)
            last.then_inc(z1_ready, 1)
            dve.wait_ge(rot0_turned, 3)
            nc.vector.tensor_tensor(z1[0:FIELDS, 0, L1_FULL, :], x4[0:FIELDS, 0, :], rot0_ps[L1_FULL],
                                    ALU.mult).then_inc(z1_ready, 1)
            for g in range(GROUPS):
                products(0, 0, 0, 0, g)
                if g == 1:
                    first_products(1, 1)
            steps(dve, step, TILES - 1, first=1)

        @block.tensor
        def _(pe):
            pe.wait_ge(ident_ready, 1)

            def layer1(t, slot, tiles=range(L1_TILES)):
                if tiles[0] == 0:
                    pe.wait_ge(z1_ready, 2 * t + 2)
                    wait(pe, r_ready[0], t)
                for k in tiles:
                    rows_k = P128 if k < L1_FULL else FIELDS
                    for c in range(2):
                        last = nc.tensor.matmul(acc1[HID * c:HID * (c + 1), 0:CHUNK], w0_sb[0:rows_k, k, :],
                                                z1[0:rows_k, slot, k, CHUNK * c:CHUNK * (c + 1)],
                                                start=k == 0, stop=k == L1_TILES - 1)
                if tiles[-1] == L1_TILES - 1:
                    last.then_inc(l1_done, 1)

            weights = (w1_sb, w2_sb)

            def both_layers(p, bank, g):
                pe.wait_ge(z_ready[0], GROUPS * (p - 3) + g + 1)
                pe.wait_ge(z_ready[1], GROUPS * (p - 5) + g + 1)
                for v in range(GROUP):
                    k = GROUP * g + v
                    for n in range(2):
                        last = nc.tensor.matmul(acc[bank][HID * n:HID * (n + 1), :], weights[n][:, k, :],
                                                z[:, n, g % 2, v, :], start=k == 0, stop=k == 2 * MT - 1)
                        if v == GROUP - 1:
                            last.then_inc(z_used[n], 1)

            def one_layer(n, t, bank, g):
                pe.wait_ge(z_ready[n], GROUPS * t + g + 1)
                for v in range(GROUP):
                    k = GROUP * g + v
                    for c in range(2):
                        last = nc.tensor.matmul(acc[bank][HID * c:HID * (c + 1), 0:CHUNK], weights[n][:, k, :],
                                                z[:, n, g % 2, v, CHUNK * c:CHUNK * (c + 1)],
                                                start=k == 0, stop=k == 2 * MT - 1)
                last.then_inc(z_used[n], 1)

            def turn(p, j):
                pe.wait_ge(rows_spread, p + 1)
                wait(pe, x4_ready, p)
                for d in range(DPP):
                    last = nc.tensor.transpose(turned[:, P128 * d:P128 * (d + 1)],
                                               rows4[:, DPP * j + d, :, :].rearrange("p g m -> p (g m)"), ident[:, :])
                last.then_inc(pair_turned, 1)

            def step(tile, j):
                p = PPT * tile + j
                if in_range(p - 3) or in_range(p - 5):
                    wait(pe, r_ready[1], min(p - 4, PAIRS) if isinstance(p, int) else p - 4)
                    wait(pe, r_ready[2], p - 6)
                for g in range(GROUPS):
                    if isinstance(tile, int) and p == PPT:
                        if g == 2:
                            layer1(2, 0)
                    elif g < GROUPS - 1 and in_range(p - 2):
                        layer1(p - 2, j % 2, range(2 * g, min(2 * g + 2, L1_TILES)))
                    if g == GROUPS - 1 and in_range(p):
                        turn(p, j)
                    if in_range(p - 3) and in_range(p - 5):
                        both_layers(p, j % 2, g)
                    elif in_range(p - 3):
                        one_layer(0, p - 3, j % 2, g)
                    elif in_range(p - 5):
                        one_layer(1, p - 5, j % 2, g)

            pe.wait_ge(tables_loaded, 16 * PICKED)
            for g in range(PICKED // 4):
                group = range(4 * g, 4 * g + 4)
                pe.wait_ge(one_hot_ready, 4 * g + 4)
                wait(pe, picked_t_ready, g - 1)
                for k in range(max(chunks)):
                    for i in group:
                        if k < chunks[i]:
                            at = DIM * (sum(chunks[:i]) + k)
                            last = nc.tensor.matmul(acc[g % 2][QUAD * (i % 4):QUAD * (i % 4) + DIM, 0:P128],
                                                    held[:, at:at + DIM], one_hot[i][:, P128 * k:P128 * (k + 1)],
                                                    start=k == 0, stop=k == chunks[i] - 1)
                last.then_inc(picked_done, 1)
                pe.wait_ge(picked_t_ready, g + 1)
                wait(pe, picked_stored, g)
                nc.tensor.transpose(turned[:, 0:P128], picked_t[:, g % 2, :], ident[:, :]).then_inc(picked_turned, 1)
            turn(0, 0)
            for k in range(L1_TILES):
                width = P128 if k < L1_FULL else FIELDS
                if k % 2 == 0 and k < L1_FULL:
                    pe.wait_ge(rot0_spread, k // 2 + 1)
                for d in range(DPP):
                    last = nc.tensor.transpose(rot0_ps[k][:, P128 * d:P128 * (d + 1)],
                                               rot0_rows[:, d, P128 * k:P128 * k + width], ident[:, :])
                if k % 2 == 1 or k == L1_FULL:
                    last.then_inc(rot0_turned, 1)
            turn(1, 1)
            turn(2, 2)
            pe.wait_ge(w0_ready, 3)
            layer1(0, 0)
            turn(3, 3)
            pe.wait_ge(cin_w_loaded[1], 16)
            pe.wait_ge(cin_w_loaded[2], 16)
            for g in range(GROUPS):
                if g == 2:
                    layer1(1, 1)
                one_layer(0, 0, 1, g)
            steps(pe, step, TILES - 1, first=1)

            pe.wait_ge(tower_loaded, 16 * 7)
            for half in range(2):
                cols = slice(HALF * half, HALF * (half + 1))
                for n in range(2):
                    pe.wait_ge(summed[n], SUMS * (TILES // 2) * (half + 1))
                for m in range(M1):
                    if half == 0:
                        pe.wait_ge(z_ready[m // 2], GROUPS * PAIRS)
                    else:
                        pe.wait_ge(h1_ready, m + 1)
                    ms = slice(P128 * m, P128 * (m + 1))
                    nc.tensor.matmul(h1_ps[m], wt1_sb[:, 0, ms], zsum[0][:, cols], start=True, stop=False)
                    nc.tensor.matmul(h1_ps[m], wt1_sb[0:HID + DIM, 1, ms], zsum[1][:, cols], start=False, stop=True)\
                        .then_inc(h1_done, 1)
            for half in range(2):
                for m in range(M2):
                    if half == 0:
                        pe.wait_ge(r_ready[2], PAIRS)
                    else:
                        pe.wait_ge(h2_ready, m + 1)
                    for k in range(M1):
                        pe.wait_ge(h1_ready, M1 * half + k + 1)
                        last = nc.tensor.matmul(h2_ps[m], wt2_sb[:, k, P128 * m:P128 * (m + 1)], h1[:, half, k, :],
                                                start=k == 0, stop=k == M1 - 1)
                    last.then_inc(h2_done, 1)
            pe.wait_ge(x4_ready, PAIRS)
            for k in range(M2):
                for half in range(2):
                    pe.wait_ge(h2_ready, M2 * half + k + 1)
                    last = nc.tensor.matmul(y_ps[half], wt3_sb[:, k:k + 1], h2[:, half, k, :], start=k == 0, stop=k == M2 - 1)
                    if k == M2 - 1:
                        last.then_inc(y_done, 1)


def rotated(w):
    m = np.arange(FIELDS)[None, :, None]
    s = np.arange(ROT)[:, None, None] + ROT * np.arange(L1_TILES)[None, None, :]
    other = (m + s) % FIELDS
    fwd = w[m, other].reshape(P128, L1_TILES, HID)
    bwd = w[other, m].reshape(P128, L1_TILES, HID)[:, :L1_FULL]
    return np.ascontiguousarray(fwd), np.ascontiguousarray(bwd)


def interleaved(w):
    q = np.arange(4)[:, None, None, None]
    hh = np.arange(QUAD)[None, :, None, None]
    u = np.arange(2)[None, None, :, None]
    v = np.arange(MT)[None, None, None, :]
    out = w[4 * v + q, QUAD * ((q + u) % 2) + hh]
    return np.ascontiguousarray(out.reshape(P128, 2 * MT, HID))


def kernel(**inputs):
    import concourse.bacc as bacc
    from concourse.bass_utils import run_bass_kernel_spmd

    a = {k: np.asarray(v) for k, v in inputs.items()}
    w0_fwd, w0_bwd = rotated(a["L0_rec_W0"])
    arrays = {
        "dense_t": np.ascontiguousarray(a["dense_ctx"].T),
        "ids": a["ids"],
        "ids_picked": np.ascontiguousarray(
            a["ids"][:P128, small_tables([a[f"tbl_{n}"].shape[0] for n in range(FIELDS)])].T),
        "w0_fwd": w0_fwd, "w0_bwd": w0_bwd,
        "w1_cin": interleaved(a["L0_rec_W1"]), "w2_cin": interleaved(a["L0_rec_W2"]),
        "w_top1": a["W_top1"],
        "b_top1": np.ascontiguousarray(a["b_top1"].reshape(M1, P128).T),
        "w_top2": np.ascontiguousarray(a["W_top2"].reshape(M1, P128, TOP2).transpose(1, 0, 2)),
        "b_top2": np.ascontiguousarray(a["b_top2"].reshape(M2, P128).T),
        "w_top3": np.ascontiguousarray(a["W_top3"].reshape(M2, P128).T),
    }
    for n in range(FIELDS):
        arrays[f"tbl_{n}"] = a[f"tbl_{n}"]
    nc = bacc.Bacc("TRN2", target_bir_lowering=False, num_devices=1)
    aps = {k: nc.dram_tensor(k, v.shape, mybir.dt.from_np(v.dtype), kind="ExternalInput").ap()
           for k, v in arrays.items()}
    y = nc.dram_tensor("y", (1, BATCH), F32, kind="ExternalOutput").ap()
    build_program(nc, aps["dense_t"], aps["ids"], aps["ids_picked"], [aps[f"tbl_{n}"] for n in range(FIELDS)],
                  aps["w0_fwd"], aps["w0_bwd"], aps["w1_cin"], aps["w2_cin"], aps["w_top1"],
                  aps["b_top1"], aps["w_top2"], aps["b_top2"], aps["w_top3"], y)
    result = run_bass_kernel_spmd(nc, [arrays], core_ids=[0])
    return result.results[0]["y"].reshape(BATCH, 1)
```

```python
from contextlib import ExitStack

import numpy as np
import concourse.bass as bass
from concourse import mybir

F32 = mybir.dt.float32
I32 = mybir.dt.int32
ALU = mybir.AluOpType
ACT = mybir.ActivationFunctionType

SUMS = 5
BATCH, FIELDS, DIM, HID = 1024, 32, 16, 64
P128 = 128
QUAD = 32
TILES = BATCH // P128
DPP = 4
PPT = DIM // DPP
PAIRS = TILES * PPT
COLS = DPP * P128
CHUNK = COLS // 2
ROT = P128 // FIELDS
L1_FULL = FIELDS // 2 // ROT
L1_TILES = L1_FULL + 1
WHEEL = FIELDS + FIELDS // 2
DVE_PAIRS = 3
MT = FIELDS // 4
GROUP = 4
GROUPS = 2 * MT // GROUP
TPC = FIELDS // PPT
TOP1, TOP2 = 512, 256
M1, M2 = TOP1 // P128, TOP2 // P128
PICKED = 19
WARM_START, WARM_PICKED, WARM_LAYER2, WARM_STEP5 = 16, 20, 28, 12
TOWER1_IN_STEP = {PAIRS + 1: {3: 0}, PAIRS + 2: {1: 1}, PAIRS + 3: {3: 2}, PAIRS + 4: {1: 3}}
HALF = BATCH // 2


def field_order(sizes):
    return sorted(range(FIELDS), key=lambda n: sizes[n])


def rows_held(size):
    held = 1
    while held * P128 < size:
        held *= 2
    return held


def packed(tables, held):
    parts = max(-(-t.shape[0] // held) for t in tables)
    out = np.zeros((parts, len(tables), held * DIM), np.float32)
    for i, t in enumerate(tables):
        flat = np.zeros(parts * held * DIM, np.float32)
        flat[:t.size] = t.reshape(-1)
        out[:, i, :] = flat.reshape(parts, held * DIM)
    return out


def build_program(nc, dense_t, ids, ids_picked, packs, tables, w0_fwd, w0_bwd, w1_cin, w2_cin,
                  w_top1, b_top1, w_top2, b_top2, w_top3, y_out):
    ctx = ExitStack()
    with ctx:
        def sb(name, shape, dt=F32):
            return ctx.enter_context(nc.sbuf_tensor(name, shape, dt))

        def pb(name, shape):
            return ctx.enter_context(nc.psum_tensor(name, shape, F32))

        def sem(name):
            return ctx.enter_context(nc.semaphore(name))

        ids_sb = sb("ids_sb", [P128, FIELDS], I32)
        rows = sb("rows", [P128, FIELDS, DIM])
        ids0_sb = sb("ids0_sb", [P128, FIELDS], I32)
        ids_wide = sb("ids_wide", [P128, PICKED * P128], I32)
        ids_low = sb("ids_low", [P128, PICKED], I32)
        rows4 = sb("rows4", [P128, DIM, 4, FIELDS])
        ident = sb("ident", [P128, P128])
        x4 = sb("x4", [P128, 2, COLS])
        rot = sb("rot", [P128, 2, L1_TILES, COLS])
        z1 = sb("z1", [P128, 2, L1_TILES, COLS])
        xb = sb("xb", [P128, PPT, MT, COLS])
        z = sb("z", [P128, 2, 2, GROUP, COLS])
        r12 = sb("r12", [P128, PPT, COLS])
        r3 = sb("r3", [HID, PPT, COLS])
        r = [r12[0:HID, :, :], r12[HID:P128, :, :], r3[:, :, :]]
        zacc = [sb("zacc12", [P128, COLS]), sb("zacc3", [HID, COLS])]
        zsum = [sb("zsum12", [P128, BATCH]), sb("zsum3d", [HID + DIM, BATCH])]
        w0_sb = sb("w0_sb", [P128, L1_TILES, HID])
        w0b_sb = sb("w0b_sb", [P128, L1_FULL, HID])
        w1_sb = sb("w1_sb", [P128, 2 * MT, HID])
        w2_sb = sb("w2_sb", [P128, 2 * MT, HID])
        wt1_sb = sb("wt1_sb", [P128, 2, TOP1])
        wt2_sb = sb("wt2_sb", [P128, M1, TOP2])
        wt3_sb = sb("wt3_sb", [P128, M2])
        bt1_sb = sb("bt1_sb", [P128, M1])
        bt2_sb = sb("bt2_sb", [P128, M2])
        rows0 = xb[:, 0, 0, :].rearrange("p (m d) -> p m d", d=DIM)
        kinds = []
        for held in sorted({rows_held(t.shape[0]) for t in tables[:PICKED]}):
            fields = [n for n in range(PICKED) if rows_held(tables[n].shape[0]) == held]
            kinds.append((held, fields[0], fields[-1] + 1))
        pack_sb, mask, at, mask_at = [], [], 0, 0
        for (held, n0, n1), pack in zip(kinds, packs):
            width, mask_width = (n1 - n0) * held * DIM, (n1 - n0) * held
            pack_sb.append(xb[0:pack.shape[0], 3, :, :].rearrange("p v n -> p (v n)")[:, at:at + width])
            mask.append(xb[:, 2, 0, mask_at:mask_at + mask_width])
            at, mask_at = at + width, mask_at + mask_width
        banks = []
        for i, (held, n0, n1) in enumerate(kinds):
            fit = COLS // (held * DIM)
            banks += [(i, n, min(n + fit, n1)) for n in range(n0, n1, fit)]
        one_hot = z[:, 0, :, :, :].rearrange("p s g n -> p (s g n)")[:, 0:PICKED * P128]
        chosen = z[:, 1, :, :, :].rearrange("p s g n -> p (s g) n")
        held_no, part_no = xb[:, 1, 0, 0:kinds[-1][0]], xb[:, 1, 1, 0:1]
        rot0_rows = z[:, 1, :, :, :].rearrange("p s g n -> p (s g n)")[:, 0:DPP * FIELDS * (FIELDS // 2 + 1)]\
            .rearrange("p (d w) -> p d w", d=DPP)
        h1 = rot[:, :, 0:M1, :]
        h2 = z1[:, :, 0:M2, :]
        y_sb = xb[0:1, 2, 0:2, :].rearrange("p h n -> p (h n)")

        wheel = nc.dram_tensor("wheel", (PPT, WHEEL, COLS), F32, kind="Internal").ap()

        xk = [pb(f"xk{n}", [P128, 2, COLS]) for n in (2, 3)]
        acc1 = pb("acc_l1", [P128, COLS])
        acc = [pb(f"acc_l23_{n}", [P128, COLS]) for n in range(2)]
        turned = pb("turned", [P128, COLS])
        candidates = [xk[0][:, 0, :], xk[0][:, 1, :], xk[1][:, 0, :], xk[1][:, 1, :]]
        rot0_ps = [xk[0][:, 0, :], xk[0][:, 1, :], xk[1][:, 0, :], xk[1][:, 1, :], acc[0][0:FIELDS, :]]
        h1_ps = [[turned[:, :], acc1[:, :], turned[:, :], acc1[:, :]],
                 [xk[1][:, 0, :], xk[1][:, 1, :], acc[0][:, :], acc[1][:, :]]]
        h2_ps = [[xk[0][:, 0, :], xk[0][:, 1, :]], [turned[:, :], acc1[:, :]]]
        y_ps = [xk[0][0:1, 0, :], xk[0][QUAD:QUAD + 1, 1, :]]

        ids_loaded = [sem(f"ids_loaded{c}") for c in range(PPT)]
        gathered = [sem(f"gathered{c}") for c in range(PPT)]
        gather_let_go = sem("gather_let_go")
        ids0_loaded = sem("ids0_loaded")
        wide_loaded = [sem(f"wide{i}_loaded") for i in range(len(packs))]
        pack_loaded = [sem(f"pack{i}_loaded") for i in range(len(packs))]
        gathered0 = sem("gathered0_rows")
        numbers_ready = sem("numbers_ready")
        low_ready = sem("low_ready")
        masks_ready = sem("masks_ready")
        high_ready = sem("high_ready")
        one_hot_ready = sem("one_hot_ready")
        candidates_ready = sem("candidates_ready")
        chosen_ready = sem("chosen_ready")
        picked_stored = sem("picked_stored")
        ident_zero, ident_ready = sem("ident_zero"), sem("ident_ready")
        cin_w_loaded = [sem("w0_loaded"), sem("w1_loaded"), sem("w2_loaded")]
        w0_ready = sem("w0_ready")
        tower_loaded = sem("tower_loaded")
        rows_spread = sem("rows_spread")
        pair_turned = sem("pair_turned")
        rot0_spread = sem("rot0_spread")
        rot0_turned = sem("rot0_turned")
        x4_ready = sem("x4_ready")
        wheel_stored = [sem(f"wheel_stored{s}") for s in range(2)]
        rot_loaded = [sem(f"rot_loaded{s}") for s in range(2)]
        xb_loaded = [sem(f"xb_loaded{s}") for s in range(PPT)]
        xb0_part_loaded = sem("xb0_part_loaded")
        z1_part_ready = sem("z1_part_ready")
        z1_ready = sem("z1_ready")
        l1_done = sem("l1_done")
        z_ready = [sem("z2_ready"), sem("z3_ready")]
        z_used = [sem("z2_used"), sem("z3_used")]
        r_ready = [sem(f"r{n}_ready") for n in (1, 2, 3)]
        xk_ready = [sem("xk2_ready"), sem("xk3_ready")]
        summed = [sem("summed12"), sem("summed3")]
        h1_done, h1_ready = sem("h1_done"), sem("h1_ready")
        h2_done, h2_ready = sem("h2_done"), sem("h2_ready")
        y_done, y_ready, y_stored = sem("y_done"), sem("y_ready"), sem("y_stored")

        def wait(eng, s, value):
            if not isinstance(value, int) or value > 0:
                eng.wait_ge(s, value)

        def in_range(t):
            return not isinstance(t, int) or 0 <= t < PAIRS

        def alone(p):
            return in_range(p - 3) != in_range(p - 5)

        def tower1_parts(p):
            return TOWER1_IN_STEP.get(p, {}) if isinstance(p, int) else {}

        def steps(eng, step, last, first=0, peeled=2):
            for tile in range(first, peeled):
                for j in range(PPT):
                    step(tile, j)
            with eng.Fori(peeled, last + 1) as tile:
                for j in range(PPT):
                    step(tile, j)
            for tile in range(last + 1, TILES + 2):
                for j in range(PPT):
                    step(tile, j)

        block = ctx.enter_context(nc.Block())

        @block.sync
        def _(sp):
            def load_ids(tile, c):
                sp.dma_start(ids_sb[:, TPC * c:TPC * (c + 1)],
                             ids[bass.ts(tile, P128), TPC * c:TPC * (c + 1)]).then_inc(ids_loaded[c], 16)

            sp.dma_start(ids0_sb[:, :], ids[0:P128, :]).then_inc(ids0_loaded, 16)
            for (held, n0, n1), loaded in zip(kinds, wide_loaded):
                src = bass.AP(ids_picked.tensor, n0 * P128, [[0, P128], [1, (n1 - n0) * P128]])
                sp.dma_start(ids_wide[:, n0 * P128:n1 * P128], src).then_inc(loaded, 16)
            for dst, src, loaded in zip(pack_sb, packs, pack_loaded):
                sp.dma_start(dst, src.rearrange("p n w -> p (n w)")).then_inc(loaded, 16)
            for c in range(PPT):
                load_ids(1, c)
            sp.dma_start(w0_sb[:, 0:L1_FULL, :], w0_fwd[:, 0:L1_FULL, :]).then_inc(cin_w_loaded[0], 16)
            sp.dma_start(w0_sb[0:FIELDS, L1_FULL, :], w0_fwd[0:FIELDS, L1_FULL, :]).then_inc(cin_w_loaded[0], 16)
            sp.dma_start(w0b_sb[:, :, :], w0_bwd).then_inc(cin_w_loaded[0], 16)
            sp.dma_start(w1_sb[:, :, :], w1_cin).then_inc(cin_w_loaded[1], 16)
            sp.dma_start(w2_sb[:, :, :], w2_cin).then_inc(cin_w_loaded[2], 16)
            for dst, src in ((wt1_sb[:, 0, :], w_top1[0:P128, :]), (wt1_sb[0:HID + DIM, 1, :], w_top1[P128:, :]),
                             (wt2_sb[:, :, :], w_top2), (wt3_sb[:, :], w_top3), (bt1_sb[:, :], b_top1),
                             (bt2_sb[:, :], b_top2), (zsum[1][HID:HID + DIM, :], dense_t)):
                sp.dma_start(dst, src).then_inc(tower_loaded, 16)

            def spread_fields(t, jj):
                wait(sp, z_ready[1], GROUPS * (t - 4) + GROUPS)
                load_xb(jj, 0, MT, xb_loaded[jj])

            def load_xb(jj, v0, v1, loaded):
                for q in range(4):
                    src = wheel[jj, 4 * v0 + q:, :]
                    src = bass.AP(src.tensor, src.offset, [[0, QUAD], [4 * COLS, v1 - v0], [1, COLS]])
                    sp.dma_start(xb[QUAD * q:QUAD * (q + 1), jj, v0:v1, :], src).then_inc(loaded, 16)

            def store_fields(tile, j):
                sp.wait_ge(x4_ready, PPT * tile + j + 1)
                sp.dma_start(wheel[j], x4[0:WHEEL, j % 2, :]).then_inc(wheel_stored[j % 2], 16)

            def wait_stored(tile, j):
                sp.wait_ge(wheel_stored[j % 2], 16 * (2 * tile + j // 2 + 1))

            def load_rotations(j):
                for g in range(ROT):
                    tiles = L1_TILES if g == 0 else L1_FULL
                    src = wheel[j, g:, :]
                    src = bass.AP(src.tensor, src.offset, [[COLS, FIELDS], [ROT * COLS, tiles], [1, COLS]])
                    sp.dma_start(rot[FIELDS * g:FIELDS * (g + 1), j % 2, 0:tiles, :], src)\
                        .then_inc(rot_loaded[j % 2], 16)

            def step(tile, j):
                t = PPT * tile + j
                if in_range(t - 2) and not (isinstance(t, int) and t < PPT + 2):
                    spread_fields(t - 2, (j - 2) % PPT)
                if in_range(t):
                    store_fields(tile, j)
                    wait_stored(tile, j)
                    load_rotations(j)
                c = (j + 2) % PPT
                nxt = tile + (1 if j < 2 else 2)
                if not isinstance(nxt, int) or 2 <= nxt < TILES:
                    sp.wait_ge(gathered[c], 16 * TPC * (nxt - 1))
                    load_ids(nxt, c)

            store_fields(0, 0)
            store_fields(0, 1)
            wait_stored(0, 0)
            load_xb(0, 0, GROUP, xb0_part_loaded)
            load_xb(0, GROUP, MT, xb_loaded[0])
            for t in range(1, PPT):
                wait_stored(0, t)
                load_rotations(t)
                if t + 1 < PPT:
                    store_fields(0, t + 1)
                    spread_fields(t, t)
            spread_fields(PPT - 1, PPT - 1)
            for c in range(2):
                sp.wait_ge(gathered[c], 16 * TPC)
                load_ids(2, c)
            steps(sp, step, TILES - 3, first=1)
            sp.wait_ge(y_ready, 2)
            sp.dma_start(y_out, y_sb).then_inc(y_stored, 16)
            sp.wait_ge(y_stored, 16)

        @block.gpsimd
        def _(pool):
            def gather(tile, c):
                pool.wait_ge(ids_loaded[c], 16 * tile)
                if not isinstance(tile, int) or tile > 1:
                    pool.wait_ge(rows_spread, PPT * tile)
                pool.sem_inc(gather_let_go, 1)
                for n in range(TPC * c, TPC * (c + 1)):
                    pool.indirect_dma_start(
                        out=rows[:, n, :], out_offset=None, in_=tables[n],
                        in_offset=bass.IndirectOffsetOnAxis(ap=ids_sb[:, n:n + 1], axis=0),
                    ).then_inc(gathered[c], 16)

            def dim_sum(n, tile, jj):
                if jj == 0:
                    return
                t = PPT * tile + jj
                out, zs = (r12, zsum[0]) if n == 0 else (r3, zsum[1][0:HID, :])
                pool.wait_ge(r_ready[n + 1], t + 1)
                wait(pool, summed[n], SUMS * tile + jj - 1)
                first = out[:, 0, :] if jj == 1 else zacc[n][:, :]
                pool.tensor_tensor(zacc[n][:, :], first, out[:, jj, :], ALU.add).then_inc(summed[n], 1)
                if jj == PPT - 1:
                    pool.wait_ge(summed[n], SUMS * tile + 3)
                    pool.tensor_tensor(zacc[n][:, 0:CHUNK], zacc[n][:, 0:CHUNK], zacc[n][:, CHUNK:COLS], ALU.add)\
                        .then_inc(summed[n], 1)
                    pool.wait_ge(summed[n], SUMS * tile + 4)
                    pool.tensor_tensor(zs[:, bass.ts(tile, P128)], zacc[n][:, 0:P128], zacc[n][:, P128:CHUNK], ALU.add)\
                        .then_inc(summed[n], 1)

            pool.iota(held_no, pattern=[[1, kinds[-1][0]]], base=0, channel_multiplier=0,
                      allow_small_or_imprecise_dtypes=True).then_inc(numbers_ready, 1)
            pool.iota(part_no, pattern=[[1, 1]], base=0, channel_multiplier=1,
                      allow_small_or_imprecise_dtypes=True).then_inc(numbers_ready, 1)
            pool.memset(ident[:, :], 0.0).then_inc(ident_zero, 1)
            pool.wait_ge(ident_zero, 1)
            pool.affine_select(out=ident[:, :], in_=ident[:, :], compare_op=ALU.not_equal, fill=1.0, base=0,
                               pattern=[[-1, P128]], channel_multiplier=1).then_inc(ident_ready, 1)
            pool.wait_ge(ids0_loaded, 16)
            for n in range(PICKED, FIELDS):
                pool.indirect_dma_start(
                    out=rows0[:, n, :], out_offset=None, in_=tables[n],
                    in_offset=bass.IndirectOffsetOnAxis(ap=ids0_sb[:, n:n + 1], axis=0),
                ).then_inc(gathered0, 16)

            def step(tile, j):
                t = PPT * tile + j - 1
                if in_range(t) and not (isinstance(t, int) and t < DVE_PAIRS):
                    slot = (j - 1) % 2
                    if isinstance(t, int) and t == DVE_PAIRS:
                        pool.wait_ge(z1_ready, 2 * DVE_PAIRS)
                    pool.wait_ge(rot_loaded[slot], 16 * ROT * (2 * tile + (j - 1) // 2 + slot))
                    pool.wait_ge(x4_ready, t + 1)
                    wait(pool, l1_done, t - 1)
                    pool.tensor_tensor(z1[:, slot, 0:L1_FULL, :],
                                       x4[:, slot, :].unsqueeze(1).broadcast_to([P128, L1_FULL, COLS]),
                                       rot[:, slot, 0:L1_FULL, :], ALU.mult).then_inc(z1_ready, 1)
                    pool.tensor_tensor(z1[0:FIELDS, slot, L1_FULL, :], x4[0:FIELDS, slot, :],
                                       rot[0:FIELDS, slot, L1_FULL, :], ALU.mult).then_inc(z1_ready, 1)
                if not isinstance(tile, int) or tile + 1 < TILES:
                    gather(tile + 1, j)
                for n in range(2):
                    lag = 4 + 2 * n
                    i, jj = tile + (j - lag) // PPT, (j - lag) % PPT
                    if not isinstance(i, int) or 0 <= i < TILES:
                        dim_sum(n, i, jj)

            steps(pool, step, TILES - 2)

        @block.scalar
        def _(act):
            def spread_rows(tile, pairs=range(PPT)):
                first = isinstance(tile, int) and tile == 0
                if first:
                    act.wait_ge(gathered0, 16 * (FIELDS - PICKED))
                    act.wait_ge(picked_stored, len(banks))
                else:
                    for c in range(PPT):
                        act.wait_ge(gathered[c], 16 * TPC * tile)
                    act.wait_ge(pair_turned, PPT * tile)
                for jj in pairs:
                    dims = slice(DPP * jj, DPP * (jj + 1))
                    src = (rows0 if first else rows)[:, :, dims].rearrange("p m d -> p d m").unsqueeze(2)
                    nc.scalar.activation(rows4[:, dims, :, :], src.broadcast_to([P128, DPP, 4, FIELDS]), ACT.Copy)\
                        .then_inc(rows_spread, 1)

            def relu(n, tile, jj, done, done_at, sums, halves):
                act.wait_ge(done, done_at)
                wait(act, summed[n // 2], SUMS * (tile - 1) + max(jj, 1))
                if halves:
                    for c in range(2):
                        last = nc.scalar.activation(r[n][:, jj, CHUNK * c:CHUNK * (c + 1)],
                                                    sums[HID * c:HID * (c + 1), 0:CHUNK], ACT.Relu)
                else:
                    side = HID * (n - 1)
                    last = nc.scalar.activation(r[n][:, jj, :], sums[side:side + HID, :], ACT.Relu)
                last.then_inc(r_ready[n], 1)

            def spread(n, t, jj, u):
                act.wait_ge(r_ready[n], t + 1)
                wait(act, z_ready[n], GROUPS * (t - 1) + GROUPS // 2 * (u + 1))
                if u == 0:
                    for q in (0, 2):
                        last = nc.scalar.activation(xk[n][QUAD * q:QUAD * (q + 2), 0, :], r[n][:, jj, :], ACT.Copy)
                else:
                    for q in range(4):
                        k0 = QUAD * ((q + 1) % 2)
                        last = nc.scalar.activation(xk[n][QUAD * q:QUAD * (q + 1), 1, :], r[n][k0:k0 + QUAD, jj, :],
                                                    ACT.Copy)
                last.then_inc(xk_ready[n], 1)

            def to_sbuf(p, tile, j):
                slot = j % 2
                act.wait_ge(pair_turned, p + 1)
                wait(act, z1_ready, 2 * (p - 2) + 2)
                wait(act, xb_loaded[j], 16 * 4 * tile)
                nc.scalar.activation(x4[:, slot, :], turned[:, :], ACT.Copy).then_inc(x4_ready, 1)

            def tower1_relu(half, m):
                if m == 0:
                    act.wait_ge(tower_loaded, 16 * 7)
                    act.wait_ge(z1_ready, 2 * (PAIRS - 1 + half))
                act.wait_ge(h1_done, M1 * half + m + 1)
                nc.scalar.activation(h1[:, half, m, :], h1_ps[half][m], ACT.Relu, bias=bt1_sb[:, m:m + 1])\
                    .then_inc(h1_ready, 1)

            nc.scalar.preload_act_table(ACT.Relu)

            def step(tile, j):
                p = PPT * tile + j
                t1, t2 = p - 2, p - 4
                if in_range(t1):
                    relu(0, tile + (j - 2) // PPT, (j - 2) % PPT, l1_done, t1 + 1, acc1, True)
                    spread(0, t1, (j - 2) % PPT, 0)
                if in_range(t2):
                    spread(1, t2, j, 0)
                late = isinstance(p, int) and p == PPT
                if in_range(p) and not late:
                    to_sbuf(p, tile, j)
                if in_range(t1):
                    spread(0, t1, (j - 2) % PPT, 1)
                if in_range(t2):
                    spread(1, t2, j, 1)
                if late:
                    spread_rows(1)
                    to_sbuf(p, tile, j)
                if j == PPT - 1 and (not isinstance(tile, int) or tile + 1 < TILES):
                    spread_rows(tile + 1)
                parts = tower1_parts(p)
                for g in parts:
                    if g < GROUPS - 1:
                        tower1_relu(0, parts[g])
                t = p - 3
                if in_range(t):
                    relu(1, tile + (j - 3) // PPT, (j - 3) % PPT, z_used[0], GROUPS * (t + 1), acc[j % 2], alone(p))
                t = p - 5
                if in_range(t):
                    relu(2, tile + (j - 5) // PPT, (j - 5) % PPT, z_used[1], GROUPS * (t + 1), acc[j % 2], alone(p))
                if GROUPS - 1 in parts:
                    tower1_relu(0, parts[GROUPS - 1])

            spread_rows(0, range(2))
            to_sbuf(0, 0, 0)
            spread_rows(0, range(2, PPT))
            to_sbuf(1, 0, 1)
            act.wait_ge(wheel_stored[0], 16)
            to_sbuf(2, 0, 2)
            relu(0, 0, 0, l1_done, 1, acc1, True)
            spread(0, 0, 0, 0)
            spread(0, 0, 0, 1)
            to_sbuf(3, 0, 3)
            relu(0, 0, 1, l1_done, 2, acc1, True)
            spread(0, 1, 1, 0)
            spread(0, 1, 1, 1)
            relu(1, 0, 0, z_used[0], GROUPS, acc[1], True)
            steps(act, step, TILES - 2, first=1, peeled=3)

            for half in range(2):
                if half == 1:
                    for m in range(M1):
                        tower1_relu(half, m)
                for m in range(M2):
                    act.wait_ge(h2_done, M2 * half + m + 1)
                    nc.scalar.activation(h2[:, half, m, :], h2_ps[half][m], ACT.Relu, bias=bt2_sb[:, m:m + 1])\
                        .then_inc(h2_ready, 1)
            act.wait_ge(y_done, 1)
            nc.scalar.activation(y_sb[:, 0:HALF], y_ps[0], ACT.Copy).then_inc(y_ready, 1)

        @block.vector
        def _(dve):
            dve.wait_ge(ids0_loaded, 16)
            for held, n0, n1 in kinds:
                nc.vector.tensor_scalar(ids_low[:, n0:n1], ids0_sb[:, n0:n1], held - 1, None, ALU.bitwise_and)\
                    .then_inc(low_ready, 1)
            dve.wait_ge(numbers_ready, 2)
            for i, (held, n0, n1) in enumerate(kinds):
                dve.wait_ge(low_ready, i + 1)
                nc.vector.tensor_tensor(mask[i].rearrange("p (n k) -> p n k", k=held),
                                        ids_low[:, n0:n1].unsqueeze(2).broadcast_to([P128, n1 - n0, held]),
                                        held_no[:, 0:held].unsqueeze(1).broadcast_to([P128, n1 - n0, held]),
                                        ALU.is_equal).then_inc(masks_ready, 1)
            for i, (held, n0, n1) in enumerate(kinds):
                part = slice(n0 * P128, n1 * P128)
                dve.wait_ge(wide_loaded[i], 16)
                nc.vector.tensor_scalar(ids_wide[:, part], ids_wide[:, part], held.bit_length() - 1, None,
                                        ALU.logical_shift_right).then_inc(high_ready, 1)
                dve.wait_ge(high_ready, i + 1)
                nc.vector.tensor_scalar(one_hot[:, part], ids_wide[:, part], part_no, None, ALU.is_equal)\
                    .then_inc(one_hot_ready, 1)

            def choose(b):
                i, n0, n1 = banks[b]
                held, first = kinds[i][0], kinds[i][1]
                own = mask[i][:, (n0 - first) * held:(n1 - first) * held]
                dve.wait_ge(candidates_ready, b + 1)
                nc.vector.tensor_tensor(
                    chosen[:, b, 0:(n1 - n0) * held * DIM].rearrange("p (k d) -> p k d", d=DIM),
                    candidates[b % 4][:, 0:(n1 - n0) * held * DIM].rearrange("p (k d) -> p k d", d=DIM),
                    own.unsqueeze(2).broadcast_to([P128, (n1 - n0) * held, DIM]), ALU.mult).then_inc(chosen_ready, 1)

            def add_up(b):
                i, n0, n1 = banks[b]
                held = kinds[i][0]
                dve.wait_ge(chosen_ready, b + 1)
                nc.vector.tensor_reduce(
                    rows0[:, n0:n1, :],
                    chosen[:, b, 0:(n1 - n0) * held * DIM].rearrange("p (n k d) -> p n d k", k=held, d=DIM),
                    mybir.AxisListType.X, ALU.add).then_inc(picked_stored, 1)

            dve.wait_ge(masks_ready, len(kinds))
            choose(0)
            for b in range(1, len(banks)):
                choose(b)
                add_up(b - 1)
            add_up(len(banks) - 1)
            dve.wait_ge(cin_w_loaded[0], 48)
            for lo, hi, a in ((QUAD, 2 * QUAD, 0), (2 * QUAD, P128, 0), (0, P128, 1)):
                b = L1_FULL if a else 1
                nc.vector.tensor_tensor(w0_sb[lo:hi, a:b, :], w0_sb[lo:hi, a:b, :], w0b_sb[lo:hi, a:b, :],
                                        ALU.add).then_inc(w0_ready, 1)

            def products(n, t, s, tile_s, g):
                u, v0 = g // 2, GROUP * (g % 2)
                if isinstance(t, int) and t == 0 and n == 0 and g == 0:
                    dve.wait_ge(xb0_part_loaded, 16 * 4)
                elif g == 0 or (isinstance(t, int) and t == 0 and n == 0 and g == 1):
                    dve.wait_ge(xb_loaded[s], 16 * 4 * (tile_s + 1))
                if g % 2 == 0:
                    dve.wait_ge(xk_ready[n], 2 * t + u + 1)
                wait(dve, z_used[n], GROUPS * t + g - 1)
                nc.vector.tensor_tensor(z[:, n, g % 2, :, :], xb[:, s, v0:v0 + GROUP, :],
                                        xk[n][:, u, :].unsqueeze(1).broadcast_to([P128, GROUP, COLS]),
                                        ALU.mult).then_inc(z_ready[n], 1)

            def first_products(t, slot):
                dve.wait_ge(rot_loaded[slot], 16 * ROT * (t // 2 + slot))
                dve.wait_ge(x4_ready, t + 1)
                wait(dve, l1_done, t - 1)
                nc.vector.tensor_tensor(z1[:, slot, 0:L1_FULL, :],
                                        x4[:, slot, :].unsqueeze(1).broadcast_to([P128, L1_FULL, COLS]),
                                        rot[:, slot, 0:L1_FULL, :], ALU.mult).then_inc(z1_ready, 1)
                nc.vector.tensor_tensor(z1[0:FIELDS, slot, L1_FULL, :], x4[0:FIELDS, slot, :],
                                        rot[0:FIELDS, slot, L1_FULL, :], ALU.mult).then_inc(z1_ready, 1)

            def step(tile, j):
                for g in range(GROUPS):
                    for n, lag in ((0, 3), (1, 5)):
                        t = PPT * tile + j - lag
                        if in_range(t):
                            products(n, t, (j - lag) % PPT, tile + (j - lag) // PPT, g)
                    if isinstance(tile, int) and PPT * tile + j == PPT and g == 1:
                        first_products(2, 0)

            dve.wait_ge(rows_spread, 1)
            for s0, s1 in ((0, 2 * ROT), (2 * ROT, FIELDS // 2 + 1)):
                src = rows4[:, 0:DPP, 0, s0:]
                src = bass.AP(src.tensor, src.offset, [list(src.ap[0]), list(src.ap[1]), [1, s1 - s0], [1, FIELDS]])
                dst = rot0_rows[:, :, FIELDS * s0:FIELDS * s1].rearrange("p d (s m) -> p d s m", m=FIELDS)
                nc.vector.tensor_copy(dst, src).then_inc(rot0_spread, 1)
            dve.wait_ge(x4_ready, 1)
            for n in range(2):
                dve.wait_ge(rot0_turned, n + 1)
                last = nc.vector.tensor_tensor(z1[:, 0, 2 * n:2 * n + 2, :],
                                               x4[:, 0, :].unsqueeze(1).broadcast_to([P128, 2, COLS]),
                                               xk[n][:, :, :], ALU.mult)
                last.then_inc(z1_ready if n else z1_part_ready, 1)
            dve.wait_ge(rot0_turned, 3)
            nc.vector.tensor_tensor(z1[0:FIELDS, 0, L1_FULL, :], x4[0:FIELDS, 0, :], rot0_ps[L1_FULL],
                                    ALU.mult).then_inc(z1_ready, 1)
            for g in range(GROUPS):
                products(0, 0, 0, 0, g)
                if g == 1:
                    first_products(1, 1)
            steps(dve, step, TILES - 1, first=1)
            dve.wait_ge(y_done, 2)
            nc.vector.tensor_copy(y_sb[:, HALF:BATCH], y_ps[1]).then_inc(y_ready, 1)

        @block.tensor
        def _(pe):
            pe.wait_ge(ident_ready, 1)

            def tower1(half, m):
                if m == 0:
                    if half == 0:
                        pe.wait_ge(tower_loaded, 16 * 7)
                    for n in range(2):
                        pe.wait_ge(summed[n], SUMS * (TILES // 2) * (half + 1))
                if half == 0:
                    if m == 0:
                        pe.wait_ge(x4_ready, PAIRS)
                    elif m == 1:
                        pe.wait_ge(r_ready[0], PAIRS)
                    else:
                        pe.wait_ge(h1_ready, m - 1)
                elif m == 0:
                    pe.wait_ge(z_ready[1], GROUPS * PAIRS)
                    pe.wait_ge(r_ready[2], PAIRS)
                cols = slice(HALF * half, HALF * (half + 1))
                ms = slice(P128 * m, P128 * (m + 1))
                nc.tensor.matmul(h1_ps[half][m], wt1_sb[:, 0, ms], zsum[0][:, cols], start=True, stop=False)
                nc.tensor.matmul(h1_ps[half][m], wt1_sb[0:HID + DIM, 1, ms], zsum[1][:, cols], start=False, stop=True)\
                    .then_inc(h1_done, 1)

            def tower2(half):
                if half == 0:
                    pe.wait_ge(z_ready[0], GROUPS * PAIRS)
                for m in range(M2):
                    for k in range(M1):
                        pe.wait_ge(h1_ready, M1 * half + k + 1)
                        last = nc.tensor.matmul(h2_ps[half][m], wt2_sb[:, k, P128 * m:P128 * (m + 1)],
                                                h1[:, half, k, :], start=k == 0, stop=k == M1 - 1)
                    last.then_inc(h2_done, 1)

            def keep_warm(count, bank):
                for _ in range(count):
                    nc.tensor.matmul(bank[:, 0:P128], ident[:, :], ident[:, :], start=True, stop=True)

            def layer1(t, slot, tiles=range(L1_TILES)):
                if tiles[0] == 0:
                    if isinstance(t, int) and t == 0:
                        pe.wait_ge(z1_part_ready, 1)
                    else:
                        pe.wait_ge(z1_ready, 2 * t + 2)
                    wait(pe, r_ready[0], t)
                for k in tiles:
                    rows_k = P128 if k < L1_FULL else FIELDS
                    for c in range(2):
                        last = nc.tensor.matmul(acc1[HID * c:HID * (c + 1), 0:CHUNK], w0_sb[0:rows_k, k, :],
                                                z1[0:rows_k, slot, k, CHUNK * c:CHUNK * (c + 1)],
                                                start=k == 0, stop=k == L1_TILES - 1)
                if tiles[-1] == L1_TILES - 1:
                    last.then_inc(l1_done, 1)

            weights = (w1_sb, w2_sb)

            def both_layers(p, bank, g):
                pe.wait_ge(z_ready[0], GROUPS * (p - 3) + g + 1)
                pe.wait_ge(z_ready[1], GROUPS * (p - 5) + g + 1)
                for v in range(GROUP):
                    k = GROUP * g + v
                    for n in range(2):
                        last = nc.tensor.matmul(acc[bank][HID * n:HID * (n + 1), :], weights[n][:, k, :],
                                                z[:, n, g % 2, v, :], start=k == 0, stop=k == 2 * MT - 1)
                        if v == GROUP - 1:
                            last.then_inc(z_used[n], 1)

            def one_layer(n, t, bank, g):
                pe.wait_ge(z_ready[n], GROUPS * t + g + 1)
                for v in range(GROUP):
                    k = GROUP * g + v
                    for c in range(2):
                        last = nc.tensor.matmul(acc[bank][HID * c:HID * (c + 1), 0:CHUNK], weights[n][:, k, :],
                                                z[:, n, g % 2, v, CHUNK * c:CHUNK * (c + 1)],
                                                start=k == 0, stop=k == 2 * MT - 1)
                last.then_inc(z_used[n], 1)

            def turn(p, j):
                pe.wait_ge(rows_spread, p + 1)
                wait(pe, x4_ready, p)
                for d in range(DPP):
                    last = nc.tensor.transpose(turned[:, P128 * d:P128 * (d + 1)],
                                               rows4[:, DPP * j + d, :, :].rearrange("p g m -> p (g m)"), ident[:, :])
                last.then_inc(pair_turned, 1)

            def step(tile, j):
                p = PPT * tile + j
                if in_range(p - 3) or in_range(p - 5):
                    wait(pe, r_ready[1], min(p - 4, PAIRS) if isinstance(p, int) else p - 4)
                    wait(pe, r_ready[2], p - 6)
                if isinstance(p, int) and p == PPT + 1:
                    keep_warm(WARM_STEP5, turned)
                for g in range(GROUPS):
                    if isinstance(tile, int) and p < PPT + 2:
                        if g == 2:
                            layer1(p - 2, j % 2)
                    elif g < GROUPS - 1 and in_range(p - 2):
                        layer1(p - 2, j % 2, range(2 * g, min(2 * g + 2, L1_TILES)))
                    if g == GROUPS - 1 and in_range(p) and not (isinstance(p, int) and p == PPT):
                        turn(p, j)
                    if isinstance(p, int) and p == PPT + 1 and g == 1:
                        turn(PPT, 0)
                    if in_range(p - 3) and in_range(p - 5):
                        both_layers(p, j % 2, g)
                    elif in_range(p - 3):
                        one_layer(0, p - 3, j % 2, g)
                    elif in_range(p - 5):
                        one_layer(1, p - 5, j % 2, g)
                    if g in tower1_parts(p):
                        tower1(0, tower1_parts(p)[g])

            keep_warm(WARM_START, acc1)
            for b, (i, n0, n1) in enumerate(banks):
                held, first = kinds[i][0], kinds[i][1]
                pe.wait_ge(one_hot_ready, i + 1)
                pe.wait_ge(pack_loaded[i], 16)
                wait(pe, chosen_ready, b - 3)
                for n in range(n0, n1):
                    width = held * DIM
                    last = nc.tensor.matmul(candidates[b % 4][:, (n - n0) * width:(n - n0 + 1) * width],
                                            one_hot[0:packs[i].shape[0], P128 * n:P128 * (n + 1)],
                                            pack_sb[i][:, (n - first) * width:(n - first + 1) * width],
                                            start=True, stop=True)
                last.then_inc(candidates_ready, 1)
            keep_warm(WARM_PICKED, acc1)
            turn(0, 0)
            for k in range(L1_TILES):
                width = P128 if k < L1_FULL else FIELDS
                if k % 2 == 0 and k < L1_FULL:
                    pe.wait_ge(rot0_spread, k // 2 + 1)
                for d in range(DPP):
                    last = nc.tensor.transpose(rot0_ps[k][:, P128 * d:P128 * (d + 1)],
                                               rot0_rows[:, d, P128 * k:P128 * k + width], ident[:, :])
                if k % 2 == 1 or k == L1_FULL:
                    last.then_inc(rot0_turned, 1)
                if k == 1:
                    turn(1, 1)
            turn(2, 2)
            pe.wait_ge(w0_ready, 3)
            layer1(0, 0, range(2))
            pe.wait_ge(z1_ready, 2)
            layer1(0, 0, range(2, L1_TILES))
            turn(3, 3)
            keep_warm(WARM_LAYER2, acc[0])
            pe.wait_ge(cin_w_loaded[1], 16)
            pe.wait_ge(cin_w_loaded[2], 16)
            for g in range(GROUPS):
                if g == 2:
                    layer1(1, 1)
                one_layer(0, 0, 1, g)
            steps(pe, step, TILES - 1, first=1)

            tower2(0)
            for m in range(M1):
                tower1(1, m)
            tower2(1)
            for k in range(M2):
                for half in range(2):
                    pe.wait_ge(h2_ready, M2 * half + k + 1)
                    last = nc.tensor.matmul(y_ps[half], wt3_sb[:, k:k + 1], h2[:, half, k, :],
                                            start=k == 0, stop=k == M2 - 1)
                    if k == M2 - 1:
                        last.then_inc(y_done, 1)


def rotated(w):
    m = np.arange(FIELDS)[None, :, None]
    s = np.arange(ROT)[:, None, None] + ROT * np.arange(L1_TILES)[None, None, :]
    other = (m + s) % FIELDS
    fwd = w[m, other].reshape(P128, L1_TILES, HID)
    bwd = w[other, m].reshape(P128, L1_TILES, HID)[:, :L1_FULL]
    return np.ascontiguousarray(fwd), np.ascontiguousarray(bwd)


def interleaved(w):
    q = np.arange(4)[:, None, None, None]
    hh = np.arange(QUAD)[None, :, None, None]
    u = np.arange(2)[None, None, :, None]
    v = np.arange(MT)[None, None, None, :]
    out = w[4 * v + q, QUAD * ((q + u) % 2) + hh]
    return np.ascontiguousarray(out.reshape(P128, 2 * MT, HID))


def kernel(**inputs):
    import concourse.bacc as bacc
    from concourse.bass_utils import run_bass_kernel_spmd

    a = {k: np.asarray(v) for k, v in inputs.items()}
    order = field_order([a[f"tbl_{n}"].shape[0] for n in range(FIELDS)])
    tables = [a[f"tbl_{n}"] for n in order]
    w0_fwd, w0_bwd = rotated(a["L0_rec_W0"][order][:, order])
    arrays = {
        "dense_t": np.ascontiguousarray(a["dense_ctx"].T),
        "ids": np.ascontiguousarray(a["ids"][:, order]),
        "ids_picked": np.ascontiguousarray(a["ids"][:P128, order[:PICKED]].T),
        "w0_fwd": w0_fwd, "w0_bwd": w0_bwd,
        "w1_cin": interleaved(a["L0_rec_W1"][order]), "w2_cin": interleaved(a["L0_rec_W2"][order]),
        "w_top1": a["W_top1"],
        "b_top1": np.ascontiguousarray(a["b_top1"].reshape(M1, P128).T),
        "w_top2": np.ascontiguousarray(a["W_top2"].reshape(M1, P128, TOP2).transpose(1, 0, 2)),
        "b_top2": np.ascontiguousarray(a["b_top2"].reshape(M2, P128).T),
        "w_top3": np.ascontiguousarray(a["W_top3"].reshape(M2, P128).T),
    }
    kinds = sorted({rows_held(t.shape[0]) for t in tables[:PICKED]})
    for i, held in enumerate(kinds):
        arrays[f"pack_{i}"] = packed([t for t in tables[:PICKED] if rows_held(t.shape[0]) == held], held)
    for n in range(FIELDS):
        arrays[f"tbl_{n}"] = tables[n]
    nc = bacc.Bacc("TRN2", target_bir_lowering=False, num_devices=1)
    aps = {k: nc.dram_tensor(k, v.shape, mybir.dt.from_np(v.dtype), kind="ExternalInput").ap()
           for k, v in arrays.items()}
    y = nc.dram_tensor("y", (1, BATCH), F32, kind="ExternalOutput").ap()
    build_program(nc, aps["dense_t"], aps["ids"], aps["ids_picked"],
                  [aps[f"pack_{i}"] for i in range(len(kinds))], [aps[f"tbl_{n}"] for n in range(FIELDS)],
                  aps["w0_fwd"], aps["w0_bwd"], aps["w1_cin"], aps["w2_cin"], aps["w_top1"],
                  aps["b_top1"], aps["w_top2"], aps["b_top2"], aps["w_top3"], y)
    result = run_bass_kernel_spmd(nc, [arrays], core_ids=[0])
    return result.results[0]["y"].reshape(BATCH, 1)
```
